# Optimizing a Trainium2 kernel written in Bass

```python
import numpy as np
import jax
import jax.numpy as jnp

def _softmax(x, axis=-1):
    return jax.nn.softmax(x, axis=axis)

def _gelu(x):
    return jax.nn.gelu(x, approximate=True)

def _silu(x):
    return jax.nn.silu(x)

def _sigmoid(x):
    return jax.nn.sigmoid(x)

def _layernorm(x, axis=-1, eps=1e-05):
    m = jnp.mean(x, axis=axis, keepdims=True)
    v = jnp.var(x, axis=axis, keepdims=True)
    return (x - m) / jnp.sqrt(v + eps)

def _scatter_add(tgt, idx, src, axis=0):
    return tgt.at[idx].add(src)

def _segment_sum(src, seg, n):
    return jax.ops.segment_sum(src, seg, n)
kernel_name = 'mk_flamingo_gated_d1_seqx_r4_cf50c5'

def setup_inputs(seed: int=0):
    np.random.seed(seed)
    _w = jnp.asarray

    def _rec_inputs():
        import jax
        import jax.numpy as jnp
        _rk = jax.random.key(seed)
        x = 7.22e-05 + 1 * jax.random.normal(jax.random.fold_in(_rk, 1), (8, 256, 512), jnp.float32)
        _lenS = 256 - jax.random.randint(jax.random.fold_in(_rk, 7), (8,), 0, max(1, 256 // 4) + 1, jnp.int32)
        _lenS2 = 256 - jax.random.randint(jax.random.fold_in(_rk, 8), (8,), 0, max(1, 256 // 4) + 1, jnp.int32)
        _ctx_2048P = jax.random.normal(jax.random.fold_in(_rk, 11), (8, 16, 512), jnp.float32)
        _ctx_2048c = jax.random.dirichlet(jax.random.fold_in(_rk, 511), 0.3 * jnp.ones((16,), jnp.float32), (8, 256))
        _ctx_2048t = jnp.einsum('bsk,bkd->bsd', _ctx_2048c, _ctx_2048P)
        _ctx_2048t = _ctx_2048t * jax.lax.rsqrt(jnp.mean(jnp.square(_ctx_2048t)) + 1e-12) * 0.953939
        ctx_2048 = 4.13588e-05 + 0.999923 * (_ctx_2048t + 0.3 * jax.random.normal(jax.random.fold_in(_rk, 611), (8, 256, 512), jnp.float32))
        _g = jax.random.normal(jax.random.fold_in(_rk, 9001), (2, 1), jnp.float32)
        _g = jnp.sign(_g) * jnp.maximum(jnp.abs(_g), 1.0) + (_g == 0) * 1.0
        g_xattn = _g[0]
        g_ffn = _g[1]
        return (x, ctx_2048, g_xattn, g_ffn)
    x, ctx_2048, g_xattn, g_ffn = _rec_inputs()

    def _L0_xattn_setup():
        import jax, jax.numpy as jnp
        import numpy as np
        import math
        EMBED = 512
        HEADS = 32
        GROUPS = 8
        GROUP_HEADS = HEADS // GROUPS
        HEAD_DIM = EMBED // HEADS
        B, S = (4, 256)
        key = jax.random.key(seed)
        ks = jax.random.split(key, 8)
        sc = 0.02
        return {'q': jax.random.normal(ks[0], (B, S, EMBED), jnp.float32), 'k': jax.random.normal(ks[1], (B, S, EMBED), jnp.float32), 'v': jax.random.normal(ks[2], (B, S, EMBED), jnp.float32), 'Wq': jax.random.normal(ks[3], (EMBED, EMBED), jnp.float32) * sc, 'Wk': jax.random.normal(ks[4], (GROUPS * HEAD_DIM, EMBED), jnp.float32) * sc, 'Wv': jax.random.normal(ks[5], (GROUPS * HEAD_DIM, EMBED), jnp.float32) * sc, 'Wfc': jax.random.normal(ks[6], (EMBED, EMBED), jnp.float32) * sc, 'bfc': jnp.zeros((EMBED,), jnp.float32)}
    _L0_xattn_all = _L0_xattn_setup()
    _L0_xattn_in = {k: v for k, v in _L0_xattn_all.items() if k in ('Wq', 'Wk', 'Wv', 'Wfc', 'bfc')}
    del _L0_xattn_all

    def _L0_ffn_setup():
        import jax, jax.numpy as jnp
        import numpy as np
        HIDDEN = 512
        INTER = 2048
        MOE_INTER = 256
        N_ROUTED = 8
        NUM_LOCAL = 8
        TOP_K = 2
        B, S = (4, 512)

        def _mlp(x, gw, uw, dw):
            g = x @ gw.T
            u = x @ uw.T
            return g * jax.nn.sigmoid(g) * u @ dw.T
        key = jax.random.key(seed)
        ks = jax.random.split(key, 8)
        std = 0.02
        return {'hidden_states': jax.random.normal(ks[0], (B, S, HIDDEN), jnp.float32), 'router_weight': jax.random.normal(ks[1], (N_ROUTED, HIDDEN), jnp.float32) * std, 'sh_gate': jax.random.normal(ks[2], (INTER, HIDDEN), jnp.float32) * std, 'sh_up': jax.random.normal(ks[3], (INTER, HIDDEN), jnp.float32) * std, 'sh_down': jax.random.normal(ks[4], (HIDDEN, INTER), jnp.float32) * std, 'r_gate': jax.random.normal(ks[5], (MOE_INTER, HIDDEN), jnp.float32) * std, 'r_up': jax.random.normal(ks[6], (MOE_INTER, HIDDEN), jnp.float32) * std, 'r_down': jax.random.normal(ks[7], (HIDDEN, MOE_INTER), jnp.float32) * std}
    _L0_ffn_all = _L0_ffn_setup()
    _L0_ffn_in = {k: v for k, v in _L0_ffn_all.items() if k in ('router_weight', 'sh_gate', 'sh_up', 'sh_down', 'r_gate', 'r_up', 'r_down')}
    del _L0_ffn_all
    return {'x': x, 'ctx_2048': ctx_2048, 'g_xattn': g_xattn, 'g_ffn': g_ffn, 'L0_xattn_Wq': _L0_xattn_in['Wq'], 'L0_xattn_Wk': _L0_xattn_in['Wk'], 'L0_xattn_Wv': _L0_xattn_in['Wv'], 'L0_xattn_Wfc': _L0_xattn_in['Wfc'], 'L0_xattn_bfc': _L0_xattn_in['bfc'], 'L0_ffn_router_weight': _L0_ffn_in['router_weight'], 'L0_ffn_sh_gate': _L0_ffn_in['sh_gate'], 'L0_ffn_sh_up': _L0_ffn_in['sh_up'], 'L0_ffn_sh_down': _L0_ffn_in['sh_down'], 'L0_ffn_r_gate': _L0_ffn_in['r_gate'], 'L0_ffn_r_up': _L0_ffn_in['r_up'], 'L0_ffn_r_down': _L0_ffn_in['r_down']}

def reference(x, ctx_2048, g_xattn, g_ffn, L0_xattn_Wq, L0_xattn_Wk, L0_xattn_Wv, L0_xattn_Wfc, L0_xattn_bfc, L0_ffn_router_weight, L0_ffn_sh_gate, L0_ffn_sh_up, L0_ffn_sh_down, L0_ffn_r_gate, L0_ffn_r_up, L0_ffn_r_down):
    import jax
    import jax.numpy as jnp

    def _L0_xattn_ref(q, k, v, Wq, Wk, Wv, Wfc, bfc):
        import jax, jax.numpy as jnp
        import numpy as np
        import math
        EMBED = 512
        HEADS = 32
        GROUPS = 8
        GROUP_HEADS = HEADS // GROUPS
        HEAD_DIM = EMBED // HEADS
        B, S = (4, 256)
        N, S_, _ = q.shape
        qh = (q @ Wq.T).reshape(N, S_, HEADS, HEAD_DIM).transpose(0, 2, 1, 3)
        kh = (k @ Wk.T).reshape(N, S_, GROUPS, HEAD_DIM).transpose(0, 2, 1, 3)
        vh = (v @ Wv.T).reshape(N, S_, GROUPS, HEAD_DIM).transpose(0, 2, 1, 3)
        kh = jnp.repeat(kh, GROUP_HEADS, axis=1)
        vh = jnp.repeat(vh, GROUP_HEADS, axis=1)
        score = jnp.einsum('bhqd,bhkd->bhqk', qh, kh) / math.sqrt(HEAD_DIM)
        attn = jax.nn.softmax(score, axis=-1)
        out = jnp.einsum('bhqk,bhkd->bhqd', attn, vh)
        out = out.transpose(0, 2, 1, 3).reshape(N, S_, EMBED)
        return out @ Wfc.T + bfc

    def _L0_ffn_ref(hidden_states, router_weight, sh_gate, sh_up, sh_down, r_gate, r_up, r_down):
        import jax, jax.numpy as jnp
        import numpy as np
        HIDDEN = 512
        INTER = 2048
        MOE_INTER = 256
        N_ROUTED = 8
        NUM_LOCAL = 8
        TOP_K = 2
        B, S = (4, 512)

        def _mlp(x, gw, uw, dw):
            g = x @ gw.T
            u = x @ uw.T
            return g * jax.nn.sigmoid(g) * u @ dw.T
        Bsz, Seq, H = hidden_states.shape
        x = hidden_states.reshape(-1, H)
        logits = x.astype(jnp.float32) @ router_weight.astype(jnp.float32).T
        topk_vals, topk_idx = jax.lax.top_k(logits, TOP_K)
        topk_w = jax.nn.softmax(topk_vals, axis=-1)
        slot_mask = (topk_idx < NUM_LOCAL).astype(topk_w.dtype)
        comb_w = jnp.sum(topk_w * slot_mask, axis=-1).astype(x.dtype)
        shared = _mlp(x, sh_gate, sh_up, sh_down)
        routed = _mlp(x, r_gate, r_up, r_down) * comb_w[:, None]
        return (shared + routed).reshape(Bsz, Seq, H)
    x = x + jnp.tanh(g_xattn[0]) * _L0_xattn_ref(_layernorm(x, axis=-1), ctx_2048, ctx_2048, L0_xattn_Wq, L0_xattn_Wk, L0_xattn_Wv, L0_xattn_Wfc, L0_xattn_bfc)
    x = x + jnp.tanh(g_ffn[0]) * _L0_ffn_ref(_layernorm(x, axis=-1), L0_ffn_router_weight, L0_ffn_sh_gate, L0_ffn_sh_up, L0_ffn_sh_down, L0_ffn_r_gate, L0_ffn_r_up, L0_ffn_r_down)
    return x

_drawn_inputs = setup_inputs


def setup_inputs(seed=0):
    import zlib

    import numpy as np

    out = dict(_drawn_inputs(seed))
    spreads = {'L0_xattn_bfc': (0.0, 0.1)}
    factors = {'L0_xattn_Wq': 8.0, 'L0_xattn_Wk': 8.0, 'L0_ffn_router_weight': 8.0}
    for name, (base, spread) in spreads.items():
        noise = np.random.default_rng([zlib.crc32(name.encode()), seed]).standard_normal(out[name].shape)
        drawn = base * np.exp(spread * noise) if base else spread * noise
        out[name] = jnp.asarray(drawn.astype(out[name].dtype))
    for name, factor in factors.items():
        out[name] = (out[name] * factor).astype(out[name].dtype)
    return out
```

```python
import numpy as np
import concourse.bass as bass
from concourse import mybir
from contextlib import ExitStack

B, S, D = 8, 256, 512
HEADS, GROUPS, DH = 32, 8, 16
SHARED, ROUTED, EXPERTS = 2048, 256, 8
P = 128
T = B * S
DC = D // P
BLOCK = 2 * S
BLOCKS = T // BLOCK
TILES = BLOCK // P
HC = P // DH
CHUNKS = HEADS // HC
STEPS = 2 * CHUNKS
RH = HEADS // GROUPS
KV = GROUPS * DH
UNITS = 8
MROW = 64
ST = MROW + 1
VW = 32
SC = 256
SECTIONS = (SHARED + ROUTED) // SC
IC = SC // P
GUW = DC * SC
SECW = 2 * GUW + IC * D
EPS = 1e-5


def build(nc, x, ctxT, wq, wk, wv, wfc, bfc, g_x, g_f, w_ffn, w_r, out):
    f32, f32r = mybir.dt.float32, mybir.dt.float32r
    ALU, ACT, AX = mybir.AluOpType, mybir.ActivationFunctionType, mybir.AxisListType
    q_scr = nc.dram_tensor("q_scr", (2, BLOCKS, CHUNKS, P, BLOCK), f32, kind="Internal").ap()
    k_scr = nc.dram_tensor("k_scr", (2, BLOCKS, P, BLOCK), f32, kind="Internal").ap()

    with ExitStack() as ctx:
        def sem(name):
            return ctx.enter_context(nc.semaphore(name))

        def sb(name, shape, dt=f32, where=ctx):
            return where.enter_context(nc.sbuf_tensor(name, shape, dt))

        xa = sb("xa", [P, T // P, D])
        ident = sb("ident", [P, P])
        tgx = sb("tgx", [P, 1])
        tgf = sb("tgf", [P, 1])
        gates = sb("gates", [P, 2])
        mv = sb("mv", [P, 2, T // P, 2])
        rstd = sb("rstd", [P, 2, T // P])
        nmr = sb("nmr", [P, 2, T // P])
        power = sb("power", [P, T // P])
        stats = sb("stats", [P, T // P, 6])
        xn = sb("xn", [P, 2, D])
        wr_raw = sb("wr_raw", [P, DC * EXPERTS])
        wr = sb("wr", [P, DC, 32])

        att = ExitStack()
        wq_h = sb("wq_h", [P, DC, D], f32r, att)
        wq_l = sb("wq_l", [P, DC, D], f32r, att)
        wkv_h = sb("wkv_h", [P, 2, DC, KV], f32r, att)
        wkv_l = sb("wkv_l", [P, 2, DC, KV], f32r, att)
        xnT_h = sb("xnT_h", [P, DC, BLOCK], f32r, att)
        xnT_l = sb("xnT_l", [P, DC, BLOCK], f32r, att)
        cx_h = sb("cx_h", [P, 2, BLOCK], f32r, att)
        cx_l = sb("cx_l", [P, 2, BLOCK], f32r, att)
        cx_raw = sb("cx_raw", [P, 2, BLOCK], f32, att)
        wfc_h = sb("wfc_h", [P, DC, D], f32r, att)
        wfc_l = sb("wfc_l", [P, DC, D], f32r, att)
        qx_h = sb("qx_h", [P, 2, BLOCK], f32r, att)
        qx_l = sb("qx_l", [P, 2, BLOCK], f32r, att)
        kx_h = sb("kx_h", [P, BLOCK], f32r, att)
        kx_l = sb("kx_l", [P, BLOCK], f32r, att)
        vT = sb("vT", [P, BLOCK], f32, att)
        vals = sb("vals", [P, 2, S // P, GROUPS, VW], f32, att)
        q_st = sb("q_st", [P, CHUNKS, HC, S], f32r, att)
        k_st = sb("k_st", [P, 2, GROUPS, S], f32r, att)
        probs = sb("probs", [P, 4, RH, S], f32, att)
        oT = sb("oT", [P, 2 * S], f32, att)
        attn = sb("attn", [P, 2 * P], f32, att)
        tbias = sb("tbias", [P, D], f32, att)
        mcol = sb("mcol", [P, 2, 16], f32, att)
        mT = sb("mT", [16, P], f32r, att)
        rden = sb("rden", [P, 16], f32, att)
        early = ExitStack()
        wfc_raw = sb("wfc_raw", [P, DC * D], f32, early)
        early.close()
        aT_h = sb("aT_h", [P, DC, S], f32r, att)
        aT_l = sb("aT_l", [P, DC, S], f32r, att)
        att.close()
        pflat = probs[:, :, :, :].rearrange("p a r s -> p (a r s)")
        wq_raw, wkv_raw = pflat[:, 0:DC * D], pflat[:, DC * D:DC * D + 2 * DC * KV]

        w_raw = sb("w_raw", [P, 2, SECW])
        w_h = [None, None]
        w_l = [None, None]
        w_h[0] = sb("w_h0", [P, SECW], f32r)
        w_l[0] = sb("w_l0", [P, SECW], f32r)
        w_h[1] = sb("w_h1", [P, SECW], f32r)
        w_l[1] = sb("w_l1", [P, SECW], f32r)
        x2T_h = sb("x2T_h", [P, DC, T], f32r)
        x2T_l = sb("x2T_l", [P, DC, T], f32r)
        hT_h = sb("hT_h", [P, 2, IC, BLOCK], f32r)
        hT_l = sb("hT_l", [P, 2, IC, BLOCK], f32r)
        silu = sb("silu", [P, IC, BLOCK])
        hid = sb("hid", [P, IC, BLOCK])
        logT = sb("logT", [P, BLOCK])
        top = sb("top", [P, T // P, EXPERTS])
        comb = sb("comb", [P, 4, T // P])

        bank = [ctx.enter_context(nc.psum_tensor(f"bank{i}", [P, 512], f32)) for i in range(8)]
        SMB, STB, OTB, TPB, PJ = bank[0:2], bank[2:4], bank[4], bank[5], bank[6:8]

        in_x = [sem(f"in_x{i}") for i in range(BLOCKS)]
        in_wkv, in_wq, in_wfc, in_small = sem("in_wkv"), sem("in_wq"), sem("in_wfc"), sem("in_small")
        in_cx = [sem("in_cx0"), sem("in_cx1")]
        in_w = [sem("in_w0"), sem("in_w1")]
        q_wr = [sem(f"q_wr{c}") for c in range(CHUNKS)]
        k_wr = sem("k_wr")
        q_rd = [sem(f"q_rd{c}") for c in range(CHUNKS)]
        k_rd = [sem("k_rd0"), sem("k_rd1")]
        m_rd = sem("m_rd")
        stored = sem("stored")
        consts, ident_ok, wq_ok, wkv_ok, wfc_ok = sem("consts"), sem("ident_ok"), sem("wq_ok"), sem("wkv_ok"), sem("wfc_ok")
        w_hi = sem("w_hi")
        gate_ok, tb_ok, passed = sem("gate_ok"), sem("tb_ok"), sem("passed")
        bn_one, bn_two, var_ok, rs_ok, nm_ok = sem("bn_one"), sem("bn_two"), sem("var_ok"), sem("rs_ok"), sem("nm_ok")
        cx_hi, cx_split, cx_used = sem("cx_hi"), sem("cx_split"), sem("cx_used")
        xn_ok, x_tr, x_hi, x_lo, xb_ok = sem("xn_ok"), sem("x_tr"), sem("x_hi"), sem("x_lo"), sem("xb_ok")
        q_pr, q_hi, q_lo = sem("q_pr"), sem("q_hi"), sem("q_lo")
        k_pr, k_hi, k_lo = sem("k_pr"), sem("k_hi"), sem("k_lo")
        v_cp, vt_tr, vt_cp = sem("v_cp"), sem("vt_tr"), sem("vt_cp")
        f_mm, f_add, ln2_one, ln2_ok = sem("f_mm"), sem("f_add"), sem("ln2_one"), sem("ln2_ok")
        sm_full, max_ok, zrow = sem("sm_full"), sem("max_ok"), sem("zrow")
        mt_tr, mt_cp = sem("mt_tr"), sem("mt_cp")
        st_full, exp_ok, pv_ok = sem("st_full"), sem("exp_ok"), sem("pv_ok")
        ot_cp, t1_tr, rden_ok, norm_ok, t2_tr, a_hi, a_lo = (sem("ot_cp"), sem("t1_tr"), sem("rden_ok"), sem("norm_ok"),
                                                             sem("t2_tr"), sem("a_hi"), sem("a_lo"))
        w_hi2, w_split, rs2_ok, nm2_ok = sem("w_hi2"), sem("w_split"), sem("rs2_ok"), sem("nm2_ok")
        xn2_ok, x2_tr, x2_hi, x2_lo = sem("xn2_ok"), sem("x2_tr"), sem("x2_hi"), sem("x2_lo")
        gu_full, silu_ok, hid_ok, h_hi, h_lo = sem("gu_full"), sem("silu_ok"), sem("hid_ok"), sem("h_hi"), sem("h_lo")
        y_full, acc_ok = sem("y_full"), sem("acc_ok")
        wr_ok, lg_mm, lg_cp, lg_tr, top_ok, comb_ok, e_ok, small = (sem("wr_ok"), sem("lg_mm"), sem("lg_cp"), sem("lg_tr"),
                                                                    sem("top_ok"), sem("comb_ok"), sem("e_ok"), sem("small"))

        block = ctx.enter_context(nc.Block())

        def blocks(eng, body):
            body(0, True, False)
            with eng.Fori(1, BLOCKS - 1) as t:
                body(t, False, False)
            body(BLOCKS - 1, False, True)

        def sections(eng, body):
            body(0, 0)
            with eng.Fori(0, (SECTIONS - 3) // 2) as i:
                body(2 * i + 1, 1)
                body(2 * i + 2, 0)
            body(SECTIONS - 2, 1)
            body(SECTIONS - 1, 0)

        @block.sync
        def _(sp):
            def r(ap):
                return ap.bitcast(f32)

            def load_cx(tb, c):
                if not (isinstance(tb, int) and tb == 0 and c < 2):
                    sp.wait_ge(cx_split, DC * tb + c - 1)
                sp.dma_start(cx_raw[:, c % 2, :], ctxT[tb, c, :, :]).then_inc(in_cx[c % 2], 16)

            def write_q(tb, oc):
                sp.wait_ge(q_hi, CHUNKS * tb + oc + 1)
                sp.wait_ge(q_lo, CHUNKS * tb + oc + 1)
                sp.dma_start(q_scr[0, tb, oc, :, :], r(qx_h[:, oc % 2, :])).then_inc(q_wr[oc], 16)
                sp.dma_start(q_scr[1, tb, oc, :, :], r(qx_l[:, oc % 2, :])).then_inc(q_wr[oc], 16)

            def read_q(tb, bb, c, n, fresh):
                if not fresh:
                    sp.wait_ge(st_full, UNITS * n)
                sp.wait_ge(q_wr[c], 32 * (tb + 1))
                for row, part in ((0, 0), (DH, 0), (2 * DH, 1)):
                    src = q_scr[part, tb, c, :, bb * S:(bb + 1) * S].rearrange("(h d) q -> d h q", d=DH)
                    sp.dma_start(r(q_st[row:row + DH, c, :, :]), src).then_inc(q_rd[c], 16)

            def write_k(tb):
                sp.wait_ge(k_hi, tb + 1)
                sp.wait_ge(k_lo, tb + 1)
                sp.dma_start(k_scr[0, tb, :, :], r(kx_h[:, :])).then_inc(k_wr, 16)
                sp.dma_start(k_scr[1, tb, :, :], r(kx_l[:, :])).then_inc(k_wr, 16)

            def read_k(tb, bb):
                sp.wait_ge(k_wr, 32 * (tb + 1))
                for row, part in ((0, 0), (DH, 1), (2 * DH, 0)):
                    src = k_scr[part, tb, :, bb * S:(bb + 1) * S].rearrange("(g d) s -> d g s", d=DH)
                    sp.dma_start(r(k_st[row:row + DH, bb, :, :]), src).then_inc(k_rd[bb], 16)

            def put_max(n, slot):
                sp.wait_ge(mt_cp, n + 1)
                for qt in range(2):
                    sp.dma_start(r(q_st[MROW:MROW + 1, slot, :, qt * P:(qt + 1) * P]),
                                 r(mT[qt * HC:(qt + 1) * HC, :])).then_inc(m_rd, 16)

            sp.dma_start(wkv_raw[:, 0:DC * KV], wk).then_inc(in_wkv, 16)
            sp.dma_start(wkv_raw[:, DC * KV:2 * DC * KV], wv).then_inc(in_wkv, 16)
            load_cx(0, 0)
            load_cx(0, 1)
            x_v = x.rearrange("(t j p) d -> t p j d", p=P, j=TILES)
            sp.dma_start(xa[:, 0:TILES, :], x_v[0]).then_inc(in_x[0], 16)
            sp.dma_start(wq_raw, wq).then_inc(in_wq, 16)
            load_cx(0, 2)
            load_cx(0, 3)
            sp.dma_start(tbias[:, :], bfc.partition_broadcast(P)).then_inc(in_small, 16)
            sp.dma_start(gates[:, 0:1], g_x.partition_broadcast(P)).then_inc(in_small, 16)
            sp.dma_start(gates[:, 1:2], g_f.partition_broadcast(P)).then_inc(in_small, 16)
            sp.dma_start(wr_raw[:, :], w_r).then_inc(in_small, 16)
            for t in range(1, BLOCKS):
                sp.dma_start(xa[:, TILES * t:TILES * (t + 1), :], x_v[t]).then_inc(in_x[t], 16)
            sp.dma_start(wfc_raw[:, :], wfc).then_inc(in_wfc, 16)
            sp.wait_ge(consts, 1)
            write_k(0)
            read_k(0, 0)
            for c in range(CHUNKS):
                write_q(0, c)
                if c < 3:
                    read_q(0, 0, c, 0, True)
            put_max(0, 0)

            def body(t, first, last):
                for s in range(STEPS):
                    n = STEPS * t + s
                    if s == 0:
                        if not first:
                            sp.wait_ge(st_full, UNITS * n)
                        read_k(t, 1)
                    if not last or s + 3 < STEPS:
                        e = s + 3
                        tb = t if e < STEPS else t + 1
                        read_q(tb, e % STEPS // CHUNKS, e % CHUNKS, n, first and s == 0)
                    if s == 1 and not last:
                        load_cx(t + 1, 0)
                        load_cx(t + 1, 1)
                    if s == 2 and not last:
                        load_cx(t + 1, 2)
                        load_cx(t + 1, 3)
                    if s == 5 and not last:
                        write_k(t + 1)
                    if not last or s + 1 < STEPS:
                        put_max(n + 1, (s + 1) % CHUNKS)
                    if not last:
                        if s == 3:
                            write_q(t + 1, 0)
                        if s == 4:
                            write_q(t + 1, 1)
                        if s == 5:
                            read_k(t + 1, 0)
                        if s == 6:
                            write_q(t + 1, 2)
                        if s == 7:
                            write_q(t + 1, 3)
                    elif s == 0:
                        sp.wait_ge(q_lo, CHUNKS * BLOCKS)
                        sp.wait_ge(k_lo, BLOCKS)
                        sp.wait_ge(v_cp, BLOCKS)
                        for sc in range(2):
                            sp.dma_start(w_raw[:, sc, :], w_ffn[sc, :, :]).then_inc(in_w[sc], 16)

            blocks(sp, body)

            def section(sc, par):
                if isinstance(sc, int) and sc + 2 >= SECTIONS:
                    return
                sp.wait_ge(w_split, sc + 1)
                sp.dma_start(w_raw[:, par, :], w_ffn[sc + 2, :, :]).then_inc(in_w[par], 16)

            body_n = SECTIONS - 2
            section(0, 0)
            with sp.Fori(0, (body_n - 1) // 2) as i:
                section(2 * i + 1, 1)
                section(2 * i + 2, 0)
            o_v = out.rearrange("(i p) d -> i p d", p=P)
            for i in range(T // P):
                sp.wait_ge(acc_ok, TILES * BLOCKS * (SECTIONS - 1) + i + 1)
                sp.dma_start(o_v[i], xa[:, i, :]).then_inc(stored, 16)
            sp.wait_ge(stored, 16 * (T // P))

        @block.gpsimd
        def _(pool):
            g = nc.gpsimd

            def split_cx(tb, c):
                pool.wait_ge(in_cx[c % 2], 16 * (2 * tb + c // 2 + 1))
                if not (isinstance(tb, int) and tb == 0 and c < 2):
                    pool.wait_ge(cx_used, DC * tb + c - 1)
                pool.sem_inc(passed)
                g.tensor_copy(cx_h[:, c % 2, :], cx_raw[:, c % 2, :]).then_inc(cx_hi, 1)
                pool.wait_ge(cx_hi, DC * tb + c + 1)
                g.tensor_tensor(cx_l[:, c % 2, :], cx_raw[:, c % 2, :], cx_h[:, c % 2, :].bitcast(f32),
                                ALU.subtract).then_inc(cx_split, 1)

            def root(lot, a, b):
                g.tensor_scalar(rstd[:, lot, a:b], mv[:, lot, a:b, 1], EPS, 0.0, ALU.add, ALU.add).then_inc(var_ok, 1)

            g.memset(ident[:, :], 0.0).then_inc(small, 1)
            pool.wait_ge(small, 1)
            g.affine_select(out=ident[:, :], in_=ident[:, :], compare_op=ALU.not_equal, fill=1.0, base=0,
                            pattern=[[-1, P]], channel_multiplier=1).then_inc(ident_ok, 1)
            g.memset(power[:, :], -0.5)
            split_cx(0, 0)
            split_cx(0, 1)
            pool.wait_ge(cx_split, 2)
            g.memset(k_st[32:64, :, :, :].bitcast(f32), 0.0).then_inc(small, 1)
            pool.wait_ge(small, 2)
            g.memset(k_st[MROW:ST, :, :, :].bitcast(f32), 1.0).then_inc(small, 1)
            pool.wait_ge(small, 3)
            g.memset(q_st[32:64, :, :, :].bitcast(f32), 0.0).then_inc(small, 1)
            pool.wait_ge(small, 4)
            g.memset(q_st[MROW:ST, :, :, :].bitcast(f32), 0.0).then_inc(small, 1)
            pool.wait_ge(small, 5)
            g.memset(vals[:, :, :, :, DH:VW], 1.0).then_inc(consts, 1)

            roots = 0
            for t in range(BLOCKS):
                if t == 1:
                    split_cx(0, 2)
                    split_cx(0, 3)
                pool.wait_ge(bn_two, TILES * (t + 1))
                root(0, TILES * t, TILES * (t + 1))
                roots += 1
                pool.wait_ge(var_ok, roots)
                g.tensor_tensor(rstd[:, 0, TILES * t:TILES * (t + 1)], rstd[:, 0, TILES * t:TILES * (t + 1)],
                                power[:, 0:TILES], ALU.pow).then_inc(rs_ok, 1)

            def add_bias(tb):
                pool.wait_ge(tb_ok, 1)
                for j in range(TILES):
                    pool.wait_ge(xn_ok, TILES * tb + j + 1)
                    tile = xa[:, bass.ds(TILES * tb + j, 1), :].rearrange("p a d -> p (a d)")
                    g.tensor_tensor(tile, tile, tbias[:, :], ALU.add).then_inc(xb_ok, 1)
                pool.wait_ge(xb_ok, TILES * (tb + 1))

            add_bias(0)

            def body(t, first, last):
                for s in range(STEPS):
                    n = STEPS * t + s
                    if not last or s + 3 < STEPS:
                        if not (first and s == 0):
                            pool.wait_ge(st_full, UNITS * n)
                        pool.sem_inc(passed)
                        g.memset(q_st[MROW:ST, (s + 3) % CHUNKS, :, :].bitcast(f32), 0.0).then_inc(zrow, 1)
                        pool.wait_ge(zrow, n + 1)
                    if last:
                        continue
                    if s == 2:
                        split_cx(t + 1, 0)
                        split_cx(t + 1, 1)
                    if s == 3:
                        add_bias(t + 1)
                    if s == 4:
                        split_cx(t + 1, 2)
                        split_cx(t + 1, 3)
                    if s in (2, 4):
                        pool.wait_ge(cx_split, DC * (t + 1) + s)
                if last:
                    split_w(0, 0)

            def split_w(sc, par):
                pool.wait_ge(in_w[par], 8 * (sc - par) + 16)
                if isinstance(sc, int) and sc == 0:
                    pool.wait_ge(q_lo, CHUNKS * BLOCKS)
                    pool.wait_ge(v_cp, BLOCKS)
                if isinstance(sc, int) and sc == 1:
                    pool.wait_ge(f_add, TILES * BLOCKS)
                    pool.wait_ge(a_lo, STEPS * BLOCKS)
                if not isinstance(sc, int) or sc >= 2:
                    pool.wait_ge(y_full, TILES * BLOCKS * (sc - 1))
                pool.sem_inc(passed)
                g.tensor_copy(w_h[par][:, :], w_raw[:, par, :]).then_inc(w_hi2, 1)
                pool.wait_ge(w_hi2, sc + 1)
                g.tensor_tensor(w_l[par][:, :], w_raw[:, par, :], w_h[par][:, :].bitcast(f32),
                                ALU.subtract).then_inc(w_split, 1)

            blocks(pool, body)
            r2 = 0
            for a, b in ((0, 12), (12, 16)):
                pool.wait_ge(ln2_ok, b)
                root(1, a, b)
                roots += 1
                r2 += 1
                pool.wait_ge(var_ok, roots)
                g.tensor_tensor(rstd[:, 1, a:b], rstd[:, 1, a:b], power[:, 0:b - a], ALU.pow).then_inc(rs2_ok, 1)
            split_w(1, 1)
            with pool.Fori(0, (SECTIONS - 3) // 2) as i:
                split_w(2 * i + 2, 0)
                split_w(2 * i + 3, 1)
            split_w(SECTIONS - 1, 0)

        @block.scalar
        def _(act):
            def copy(out, in_):
                return nc.scalar.activation(out, in_, ACT.Copy)

            def normalise(lot, i, slot):
                tile = xa[:, bass.ds(i, 1), :].rearrange("p a d -> p (a d)")
                return nc.scalar.activation(xn[:, slot, :], tile, ACT.Identity,
                                            bias=nmr[:, lot, bass.ds(i, 1)], scale=rstd[:, lot, bass.ds(i, 1)])

            def xn_tile(tb, j):
                if not (isinstance(tb, int) and tb == 0 and j < 2):
                    act.wait_ge(x_tr, TILES * tb + j - 1)
                normalise(0, TILES * tb + j, j % 2).then_inc(xn_ok, 1)

            def x_high(tb, j, bk):
                act.wait_ge(x_tr, TILES * tb + j + 1)
                if not (isinstance(tb, int) and tb == 0):
                    act.wait_ge(q_pr, CHUNKS * tb)
                copy(xnT_h[:, :, j * P:(j + 1) * P], PJ[bk][:, :].rearrange("p (c q) -> p c q", c=DC)).then_inc(x_hi, 1)

            def q_high(tb, oc):
                act.wait_ge(q_pr, CHUNKS * tb + oc + 1)
                if isinstance(tb, int) and tb == 0:
                    if oc >= 2:
                        act.wait_ge(q_wr[oc - 2], 32)
                else:
                    act.wait_ge(q_wr[(oc + 2) % 4], 32 * (tb + 1) if oc >= 2 else 32 * tb)
                copy(qx_h[:, oc % 2, :], PJ[oc % 2][:, :]).then_inc(q_hi, 1)

            def k_high(tb):
                act.wait_ge(k_pr, tb + 1)
                if not (isinstance(tb, int) and tb == 0):
                    act.wait_ge(k_wr, 32 * tb)
                copy(kx_h[:, :], PJ[0][:, :]).then_inc(k_hi, 1)

            def v_copy(tb):
                act.wait_ge(cx_used, DC * (tb + 1))
                if not (isinstance(tb, int) and tb == 0):
                    act.wait_ge(vt_tr, 2 * tb)
                copy(vT[:, :], PJ[1][:, :]).then_inc(v_cp, 1)

            def vt_copy(tb, bb):
                act.wait_ge(vt_tr, 2 * tb + bb + 1)
                if not (isinstance(tb, int) and tb == 0):
                    act.wait_ge(pv_ok, 4 * (STEPS * (tb - 1) + CHUNKS * (bb + 1)))
                copy(vals[:, bb, :, :, 0:DH],
                     PJ[0][:, 0:S].rearrange("p (k g d) -> p k g d", k=S // P, g=GROUPS)).then_inc(vt_cp, 1)

            act.wait_ge(in_wkv, 32)
            copy(wkv_h[:, :, :, :].rearrange("p a c n -> p (a c n)"), wkv_raw).then_inc(w_hi, 1)
            act.wait_ge(in_wq, 16)
            copy(wq_h[:, :, :].rearrange("p c n -> p (c n)"), wq_raw).then_inc(w_hi, 1)
            act.wait_ge(in_small, 64)
            nc.scalar.activation(tgx[:, :], gates[:, 0:1], ACT.Tanh).then_inc(gate_ok, 1)
            nc.scalar.activation(tgf[:, :], gates[:, 1:2], ACT.Tanh).then_inc(gate_ok, 1)
            act.wait_ge(consts, 1)
            k_high(0)
            v_copy(0)
            act.wait_ge(nm_ok, 1)
            xn_tile(0, 0)
            xn_tile(0, 1)
            for j in range(TILES):
                x_high(0, j, j % 2)
                if j < 2:
                    xn_tile(0, j + 2)
            act.wait_ge(in_wfc, 16)
            copy(wfc_h[:, :, :].rearrange("p c n -> p (c n)"), wfc_raw[:, :]).then_inc(w_hi, 1)
            for oc in range(CHUNKS):
                q_high(0, oc)
            vt_copy(0, 0)
            act.wait_ge(nm_ok, BLOCKS)
            act.wait_ge(wfc_ok, 1)
            act.wait_ge(wq_ok, 1)
            act.wait_ge(wkv_ok, 1)

            def a_high(n, c, batch):
                act.wait_ge(t2_tr, n + 1)
                if not (isinstance(batch, int) and batch == 0):
                    act.wait_ge(f_mm, 2 * batch)
                copy(aT_h[:, c, :], TPB[:, 0:S]).then_inc(a_hi, 1)

            def body(t, first, last):
                for s in range(STEPS):
                    n = STEPS * t + s
                    for u in range(UNITS):
                        p = u // 2
                        act.wait_ge(st_full, UNITS * n + u + 1)
                        if u % 2 == 0 and not (first and s == 0):
                            act.wait_ge(pv_ok, 4 * (n - 1) + p + 1)
                        nc.scalar.activation(probs[:, p, 2 * (u % 2):2 * (u % 2) + 2, :],
                                             STB[u % 2][:, :].rearrange("p (r q) -> p r q", r=2),
                                             ACT.Exp, scale=float(DH) ** -0.5).then_inc(exp_ok, 1)
                        if u == 0 and not last:
                            if s == 1:
                                x_high(t + 1, 1, 1)
                            if s == 4:
                                q_high(t + 1, 1)
                            if s == 5:
                                k_high(t + 1)
                                v_copy(t + 1)
                            if s == 7:
                                q_high(t + 1, 3)
                        if s == 0 and not last:
                            if u == 0:
                                xn_tile(t + 1, 0)
                            if u == 2:
                                xn_tile(t + 1, 1)
                            if u == 5:
                                x_high(t + 1, 0, 0)
                        if s == 1 and u in (3, 5) and not last:
                            xn_tile(t + 1, u // 2 + 1)
                        if s == 2 and u == 1 and not last:
                            x_high(t + 1, 2, 0)
                        if s == 2 and u == 3 and not last:
                            x_high(t + 1, 3, 1)
                        if s == 2 and u == 5:
                            vt_copy(t, 1)
                        if s == 3 and u == 5 and not last:
                            q_high(t + 1, 0)
                        if s == 6 and u == 5 and not last:
                            q_high(t + 1, 2)
                        if s == 7 and u == 5 and not last:
                            vt_copy(t + 1, 0)
                    if not (first and s == 0):
                        a_high(n - 1, (s - 1) % CHUNKS, 2 * t + (s - 1) // CHUNKS)

            blocks(act, body)
            a_high(STEPS * BLOCKS - 1, CHUNKS - 1, B - 1)

            def x2_tile(i):
                if i == 0 or i == 12:
                    act.wait_ge(nm2_ok, 1 if i == 0 else 2)
                act.wait_ge(x2_tr, i - 1) if i >= 2 else None
                normalise(1, i, i % 2).then_inc(xn2_ok, 1)

            def x2_high(i):
                act.wait_ge(x2_tr, i + 1)
                copy(x2T_h[:, :, i * P:(i + 1) * P],
                     bank[4 + i % 4][:, :].rearrange("p (c q) -> p c q", c=DC)).then_inc(x2_hi, 1)

            def section(sc, par):
                head = isinstance(sc, int) and sc == 0
                if isinstance(sc, int) and sc == SECTIONS - 1:
                    act.wait_ge(top_ok, T // P)
                    act.wait_ge(comb_ok, 1)
                    nc.scalar.activation(comb[:, 1, :], comb[:, 0, :], ACT.Exp).then_inc(e_ok, 1)
                for b in range(BLOCKS):
                    k = BLOCKS * sc + b
                    if head:
                        x2_tile(TILES * b)
                        x2_tile(TILES * b + 1)
                        for j in range(TILES):
                            x2_high(TILES * b + j)
                            if j < 2:
                                x2_tile(TILES * b + j + 2)
                    for ic in range(IC):
                        act.wait_ge(gu_full, IC * k + ic + 1)
                        if not (head and b == 0):
                            act.wait_ge(hid_ok, IC * (k - 1) + ic + 1)
                        nc.scalar.activation(silu[:, ic, :], bank[2 * ic][:, :], ACT.Silu).then_inc(silu_ok, 1)
                    for ic in range(IC):
                        act.wait_ge(hid_ok, IC * k + ic + 1)
                        if not (head and b < 2):
                            act.wait_ge(y_full, TILES * (k - 1))
                        copy(hT_h[:, b % 2, ic, :], hid[:, ic, :]).then_inc(h_hi, 1)

            sections(act, section)

        @block.vector
        def _(dve):
            v = nc.vector

            def low(out, psum, high):
                return v.tensor_tensor(out, psum, high.bitcast(f32), ALU.subtract)

            def aggregate(lot, i, done):
                v.bn_aggr(mv[:, lot, i, :], stats[:, i, :]).then_inc(done, 1)

            def x_low(tb, j, bk):
                dve.wait_ge(x_hi, TILES * tb + j + 1)
                sl = slice(j * P, (j + 1) * P)
                low(xnT_l[:, :, sl], PJ[bk][:, :].rearrange("p (c q) -> p c q", c=DC), xnT_h[:, :, sl]).then_inc(x_lo, 1)

            def q_low(tb, oc):
                dve.wait_ge(q_hi, CHUNKS * tb + oc + 1)
                low(qx_l[:, oc % 2, :], PJ[oc % 2][:, :], qx_h[:, oc % 2, :]).then_inc(q_lo, 1)

            def k_low(tb):
                dve.wait_ge(k_hi, tb + 1)
                low(kx_l[:, :], PJ[0][:, :], kx_h[:, :]).then_inc(k_lo, 1)

            def maximum(n, u, par):
                qt, g2, half = u // 2 % 2, u // 4, u % 2
                dve.wait_ge(sm_full, UNITS * n + u + 1)
                if u == 0 and not (isinstance(n, int) and n < 2):
                    dve.wait_ge(mt_tr, n - 1)
                at = qt * HC + g2 * RH + half * 2
                v.tensor_reduce(mcol[:, par, at:at + 2], SMB[u % 2][:, :].rearrange("p (r k) -> p r k", r=2),
                                AX.X, ALU.max).then_inc(max_ok, 1)

            def m_copy(n):
                dve.wait_ge(mt_tr, n + 1)
                if not (isinstance(n, int) and n == 0):
                    dve.wait_ge(m_rd, 32 * n)
                v.tensor_scalar(mT[:, :], TPB[0:16, 0:P], -1.0, None, ALU.mult).then_inc(mt_cp, 1)

            def f_done(t, bb, qt):
                f = TILES * t + 2 * bb + qt
                dve.wait_ge(f_mm, f + 1)
                dve.wait_ge(xb_ok, f + 1)
                tile = xa[:, bass.ds(f, 1), :].rearrange("p a d -> p (a d)")
                v.scalar_tensor_tensor(tile, PJ[qt][:, :], tgx[:, :], tile, ALU.mult, ALU.add).then_inc(f_add, 1)
                dve.wait_ge(f_add, f + 1)
                dve.wait_ge(bn_two, T // P)
                v.bn_stats(stats[:, bass.ds(f, 1), :].rearrange("p a k -> p (a k)"), tile).then_inc(ln2_one, 1)

            dve.wait_ge(w_hi, 1)
            v.tensor_tensor(wkv_l[:, :, :, :].rearrange("p a c n -> p (a c n)"), wkv_raw,
                            wkv_h[:, :, :, :].rearrange("p a c n -> p (a c n)").bitcast(f32), ALU.subtract).then_inc(wkv_ok, 1)

            def norm_rows(t):
                dve.wait_ge(rs_ok, t + 1)
                a, b = TILES * t, TILES * (t + 1)
                v.scalar_tensor_tensor(nmr[:, 0, a:b], mv[:, 0, a:b, 0], -1.0, rstd[:, 0, a:b],
                                       ALU.mult, ALU.mult).then_inc(nm_ok, 1)

            for t in range(BLOCKS):
                dve.wait_ge(in_x[t], 16)
                for j in range(TILES):
                    i = TILES * t + j
                    v.bn_stats(stats[:, i, :], xa[:, i, :]).then_inc(bn_one, 1)
                dve.wait_ge(bn_one, TILES * (t + 1))
                for j in range(TILES):
                    aggregate(0, TILES * t + j, bn_two)
                if t == 0:
                    dve.wait_ge(w_hi, 2)
                    v.tensor_tensor(wq_l[:, :, :].rearrange("p c n -> p (c n)"), wq_raw,
                                    wq_h[:, :, :].rearrange("p c n -> p (c n)").bitcast(f32),
                                    ALU.subtract).then_inc(wq_ok, 1)
                    norm_rows(0)
                    k_low(0)
                    dve.wait_ge(gate_ok, 2)
                    v.tensor_scalar(tbias[:, :], tbias[:, :], tgx[:, :], None, ALU.mult).then_inc(tb_ok, 1)
                    for j in range(TILES):
                        x_low(0, j, j % 2)
                    dve.wait_ge(w_hi, 3)
                    v.tensor_tensor(wfc_l[:, :, :].rearrange("p c n -> p (c n)"), wfc_raw[:, :],
                                    wfc_h[:, :, :].rearrange("p c n -> p (c n)").bitcast(f32),
                                    ALU.subtract).then_inc(wfc_ok, 1)
                    for oc in range(CHUNKS):
                        q_low(0, oc)
            v.memset(wr[:, :, :], 0.0).then_inc(wr_ok, 1)
            dve.wait_ge(wr_ok, 1)
            v.tensor_copy(wr[:, :, 0:EXPERTS], wr_raw[:, :].rearrange("p (c e) -> p c e", c=DC)).then_inc(wr_ok, 1)
            for u in range(UNITS):
                maximum(0, u, 0)
            m_copy(0)
            for u in range(UNITS):
                maximum(1, u, 1)
            for t in range(1, BLOCKS):
                norm_rows(t)

            def a_low(n, c):
                dve.wait_ge(a_hi, n + 1)
                low(aT_l[:, c, :], TPB[:, 0:S], aT_h[:, c, :]).then_inc(a_lo, 1)

            def o_copy(n):
                dve.wait_ge(pv_ok, 4 * n + 4)
                v.tensor_copy(oT[:, :], OTB[:, :]).then_inc(ot_cp, 1)

            def divide(n):
                tp = TPB[:, :].rearrange("p (h w) -> p h w", w=VW)
                dve.wait_ge(t1_tr, n + 1)
                v.reciprocal(rden[:, :], tp[:, :, DH]).then_inc(rden_ok, 1)
                dve.wait_ge(rden_ok, n + 1)
                v.tensor_tensor(attn[:, :].rearrange("p (h d) -> p h d", d=DH), tp[:, :, 0:DH],
                                rden[:, :].unsqueeze(2).to_broadcast([P, 16, DH]), ALU.mult).then_inc(norm_ok, 1)

            def body(t, first, last):
                for s in range(STEPS):
                    n = STEPS * t + s
                    prev = not (first and s == 0)
                    for u in range(UNITS):
                        if not last or s + 2 < STEPS:
                            maximum(n + 2, u, s % 2)
                        if u == 0 and (not first or s > 1):
                            a_low(n - 2, (s - 2) % CHUNKS)
                        if u == 0 and s == 5 and not last:
                            k_low(t + 1)
                        if u == 1:
                            if prev:
                                o_copy(n - 1)
                            if not last:
                                if s == 1:
                                    x_low(t + 1, 1, 1)
                                if s == 4:
                                    q_low(t + 1, 1)
                                if s == 7:
                                    q_low(t + 1, 3)
                            if s == 2 and not first:
                                f_done(t - 1, 1, 1)
                            if s == 6:
                                f_done(t, 0, 1)
                        if u == 2 and (not last or s + 1 < STEPS):
                            m_copy(n + 1)
                        if u == 4 and prev:
                            divide(n - 1)
                        if s == 2 and u == 2 and not last:
                            x_low(t + 1, 2, 0)
                        if s == 2 and u == 4 and not last:
                            x_low(t + 1, 3, 1)
                        if u == 5:
                            if not last:
                                if s == 0:
                                    x_low(t + 1, 0, 0)
                                if s == 3:
                                    q_low(t + 1, 0)
                                if s == 6:
                                    q_low(t + 1, 2)
                            if s == 1 and not first:
                                f_done(t - 1, 1, 0)
                            if s == 5:
                                f_done(t, 0, 0)
                    if last and s == 3:
                        dve.wait_ge(ln2_one, TILES * t)
                        for i in range(TILES * t):
                            aggregate(1, i, ln2_ok)

            blocks(dve, body)
            N = STEPS * BLOCKS
            a_low(N - 2, CHUNKS - 2)
            o_copy(N - 1)
            divide(N - 1)
            a_low(N - 1, CHUNKS - 1)
            for i, (a, b) in enumerate(((0, 12), (12, 16))):
                if i:
                    f_done(BLOCKS - 1, 1, 0)
                    f_done(BLOCKS - 1, 1, 1)
                    dve.wait_ge(ln2_one, T // P)
                    for i2 in range(a, b):
                        aggregate(1, i2, ln2_ok)
                dve.wait_ge(rs2_ok, i + 1)
                v.scalar_tensor_tensor(nmr[:, 1, a:b], mv[:, 1, a:b, 0], -1.0, rstd[:, 1, a:b],
                                       ALU.mult, ALU.mult).then_inc(nm2_ok, 1)

            def x2_low(i):
                sl = slice(i * P, (i + 1) * P)
                dve.wait_ge(x2_hi, i + 1)
                low(x2T_l[:, :, sl], bank[4 + i % 4][:, :].rearrange("p (c q) -> p c q", c=DC),
                    x2T_h[:, :, sl]).then_inc(x2_lo, 1)

            def accumulate(k, b, routed):
                for j in range(TILES):
                    i = TILES * b + j
                    dve.wait_ge(y_full, TILES * k + j + 1)
                    scale = comb[:, 0, i:i + 1] if routed else tgf[:, :]
                    v.scalar_tensor_tensor(xa[:, i, :], bank[4 + j][:, :], scale, xa[:, i, :],
                                           ALU.mult, ALU.add).then_inc(acc_ok, 1)

            def router():
                dve.wait_ge(lg_mm, 1)
                v.tensor_copy(logT[:, :], bank[0][:, :]).then_inc(lg_cp, 1)
                dve.wait_ge(lg_tr, 1)
                lg = bank[1][:, :].rearrange("p (j b e) -> p j b e", j=TILES, b=BLOCKS)
                for b in range(BLOCKS):
                    for j in range(TILES):
                        v.max(top[:, TILES * b + j, :], lg[:, j, b, 0:EXPERTS]).then_inc(top_ok, 1)
                dve.wait_ge(top_ok, T // P)
                v.tensor_tensor(comb[:, 0, :], top[:, :, 1], top[:, :, 0], ALU.subtract).then_inc(comb_ok, 1)

            def weights():
                dve.wait_ge(e_ok, 1)
                v.tensor_scalar(comb[:, 2, :], comb[:, 1, :], 1.0, None, ALU.add).then_inc(comb_ok, 1)
                dve.wait_ge(comb_ok, 2)
                v.reciprocal(comb[:, 3, :], comb[:, 2, :]).then_inc(comb_ok, 1)
                dve.wait_ge(comb_ok, 3)
                v.tensor_tensor(comb[:, 1, :], comb[:, 1, :], comb[:, 3, :], ALU.mult).then_inc(comb_ok, 1)
                dve.wait_ge(comb_ok, 4)
                v.tensor_tensor(comb[:, 2, :], comb[:, 1, :], comb[:, 3, :], ALU.add).then_inc(comb_ok, 1)
                dve.wait_ge(comb_ok, 5)
                v.tensor_scalar(comb[:, 0, :], comb[:, 2, :], tgf[:, :], None, ALU.mult).then_inc(comb_ok, 1)
                dve.wait_ge(comb_ok, 6)

            def section(sc, par):
                head = isinstance(sc, int) and sc == 0
                tail = isinstance(sc, int) and sc == SECTIONS - 1
                if isinstance(sc, int) and sc == SECTIONS - 2:
                    router()
                for b in range(BLOCKS):
                    k = BLOCKS * sc + b
                    if head:
                        for j in range(TILES):
                            x2_low(TILES * b + j)
                    for ic in range(IC):
                        dve.wait_ge(silu_ok, IC * k + ic + 1)
                        if not (head and b == 0):
                            dve.wait_ge(h_lo, IC * (k - 1) + ic + 1)
                        v.tensor_tensor(hid[:, ic, :], bank[2 * ic + 1][:, :], silu[:, ic, :], ALU.mult).then_inc(hid_ok, 1)
                    for ic in range(IC):
                        dve.wait_ge(h_hi, IC * k + ic + 1)
                        v.tensor_tensor(hT_l[:, b % 2, ic, :], hid[:, ic, :], hT_h[:, b % 2, ic, :].bitcast(f32),
                                        ALU.subtract).then_inc(h_lo, 1)
                    if not (head and b == 0):
                        accumulate(k - 1, (b - 1) % BLOCKS, tail and b > 0)
                if tail:
                    accumulate(BLOCKS * SECTIONS - 1, BLOCKS - 1, True)

            def section_w(sc, par):
                if isinstance(sc, int) and sc == SECTIONS - 1:
                    weights()
                section(sc, par)

            sections(dve, section_w)

        @block.tensor
        def _(pe):
            mm = nc.tensor.matmul

            def three(out, a_h, a_l, b_h, b_l, start, stop):
                mm(out, a_h, b_l, start=start, stop=False)
                mm(out, a_l, b_h, start=False, stop=False)
                return mm(out, a_h, b_h, start=False, stop=stop)

            def tr(out, in_):
                return nc.tensor.transpose(out, in_, ident[:, :])

            def x_job(tb, j, bk):
                pe.wait_ge(xn_ok, TILES * tb + j + 1)
                for c in range(DC):
                    last = tr(PJ[bk][:, c * P:(c + 1) * P], xn[:, j % 2, c * P:(c + 1) * P])
                last.then_inc(x_tr, 1)

            def q_part(tb, oc, c):
                if c == 0:
                    pe.wait_ge(x_lo, TILES * (tb + 1))
                w = slice(oc * P, (oc + 1) * P)
                last = three(PJ[oc % 2][:, :], wq_h[:, c, w], wq_l[:, c, w], xnT_h[:, c, :], xnT_l[:, c, :],
                             c == 0, c == DC - 1)
                if c == DC - 1:
                    last.then_inc(q_pr, 1)

            def kv_part(tb, a, c):
                pe.wait_ge(cx_split, DC * tb + c + 1)
                last = three(PJ[a][:, :], wkv_h[:, a, c, :], wkv_l[:, a, c, :], cx_h[:, c % 2, :], cx_l[:, c % 2, :],
                             c == 0, c == DC - 1)
                if a == 1:
                    last.then_inc(cx_used, 1)
                elif c == DC - 1:
                    last.then_inc(k_pr, 1)

            def vt_job(tb, bb):
                pe.wait_ge(v_cp, tb + 1)
                for kt in range(S // P):
                    last = tr(PJ[0][:, kt * P:(kt + 1) * P], vT[:, bb * S + kt * P:bb * S + (kt + 1) * P])
                last.then_inc(vt_tr, 1)

            def f_part(t, bb, qt, c):
                if qt == 0:
                    pe.wait_ge(a_lo, STEPS * t + CHUNKS * bb + c + 1)
                w = slice(qt * P, (qt + 1) * P)
                last = three(PJ[qt][:, :], aT_h[:, c, w], aT_l[:, c, w], wfc_h[:, c, :], wfc_l[:, c, :],
                             c == 0, c == DC - 1)
                if c == DC - 1:
                    last.then_inc(f_mm, 1)

            def sm_unit(n, u, bb, c):
                qt, g2, half = u // 2 % 2, u // 4, u % 2
                if not (isinstance(n, int) and n == 0 and u < 2):
                    pe.wait_ge(max_ok, UNITS * n + u - 1)
                for j in range(2):
                    last = mm(SMB[u % 2][:, j * S:(j + 1) * S], q_st[0:ST, c, g2 * RH + half * 2 + j, qt * P:(qt + 1) * P],
                              k_st[0:ST, bb, 2 * c + g2, :], start=True, stop=True)
                last.then_inc(sm_full, 1)

            def st_unit(n, u, bb, c):
                g2, kt, half = u // 4, u // 2 % 2, u % 2
                if not (isinstance(n, int) and n == 0 and u < 2):
                    pe.wait_ge(exp_ok, UNITS * n + u - 1)
                h = g2 * RH + half * 2
                mm(STB[u % 2][:, :], k_st[0:ST, bb, 2 * c + g2, kt * P:(kt + 1) * P], q_st[0:ST, c, h:h + 2, :],
                   start=True, stop=True).then_inc(st_full, 1)

            def pv_unit(n, p, bb, c):
                g2, kt = p // 2, p % 2
                pe.wait_ge(exp_ok, UNITS * n + 2 * p + 2)
                if p == 0 and not (isinstance(n, int) and n == 0):
                    pe.wait_ge(ot_cp, n)
                for r in range(RH):
                    last = mm(OTB[32 * r:32 * r + VW, g2 * S:(g2 + 1) * S], vals[:, bb, kt, 2 * c + g2, :],
                              probs[:, p, r, :], start=kt == 0, stop=kt == 1)
                last.then_inc(pv_ok, 1)

            def mt_job(n, par):
                pe.wait_ge(max_ok, UNITS * n + UNITS)
                tr(TPB[0:16, 0:P], mcol[:, par, :]).then_inc(mt_tr, 1)

            def t1_job(n):
                pe.wait_ge(ot_cp, n + 1)
                for qt in range(2):
                    for g2 in range(2):
                        last = tr(TPB[:, (2 * qt + g2) * P:(2 * qt + g2 + 1) * P],
                                  oT[:, g2 * S + qt * P:g2 * S + (qt + 1) * P])
                last.then_inc(t1_tr, 1)

            def t2_job(n):
                pe.wait_ge(norm_ok, n + 1)
                for qt in range(2):
                    last = tr(TPB[:, qt * P:(qt + 1) * P], attn[:, qt * P:(qt + 1) * P])
                last.then_inc(t2_tr, 1)

            pe.wait_ge(ident_ok, 1)
            pe.wait_ge(wkv_ok, 1)
            for c in range(DC):
                kv_part(0, 0, c)
                kv_part(0, 1, c)
            pe.wait_ge(k_lo, 1)
            x_job(0, 0, 0)
            pe.wait_ge(v_cp, 1)
            x_job(0, 1, 1)
            pe.wait_ge(x_lo, 1)
            x_job(0, 2, 0)
            pe.wait_ge(x_lo, 2)
            x_job(0, 3, 1)
            pe.wait_ge(wq_ok, 1)
            for oc in range(CHUNKS):
                pe.wait_ge(x_lo, 3 + oc % 2) if oc < 2 else pe.wait_ge(q_lo, oc - 1)
                for c in range(DC):
                    q_part(0, oc, c)
            pe.wait_ge(q_lo, 3)
            vt_job(0, 0)
            pe.wait_ge(consts, 1)
            pe.wait_ge(k_rd[0], 48)
            for n in range(2):
                pe.wait_ge(q_rd[n], 48)
                for u in range(UNITS):
                    sm_unit(n, u, 0, n)
                if n == 0:
                    mt_job(0, 0)

            pe.wait_ge(wfc_ok, 1)

            def body(t, first, last):
                nx = t + 1
                for s in range(STEPS):
                    n = STEPS * t + s
                    bb, c = s // CHUNKS, s % CHUNKS
                    e = s + 2
                    te = t if e < STEPS else nx
                    be, ce = e % STEPS // CHUNKS, e % CHUNKS
                    look = not last or e < STEPS
                    for u in range(UNITS):
                        if look:
                            if u == 0:
                                pe.wait_ge(q_rd[ce], 48 * (2 * te + be + 1))
                                pe.wait_ge(k_rd[be], 48 * (te + 1))
                                if not (first and s == 0):
                                    pe.wait_ge(zrow, n)
                            sm_unit(n + 2, u, be, ce)
                        if u == 0:
                            pe.wait_ge(m_rd, 32 * (n + 1))
                        st_unit(n, u, bb, c)
                        if u == 1 and not (first and s == 0):
                            pv_unit(n - 1, 3, (s - 1) % STEPS // CHUNKS, (s - 1) % CHUNKS)
                        if u == 3 and c == 0:
                            pe.wait_ge(vt_cp, 2 * t + bb + 1)
                        if u in (3, 5, 7):
                            pv_unit(n, u // 2 - 1, bb, c)
                        if u == 2 and (not last or s + 1 < STEPS):
                            if not first or s > 1:
                                pe.wait_ge(a_lo, n - 1)
                            else:
                                pe.wait_ge(mt_cp, n + 1)
                            mt_job(n + 1, (s + 1) % 2)
                        if u == 4 and not (first and s == 0):
                            if not last or s + 1 < STEPS:
                                pe.wait_ge(mt_cp, n + 2)
                            else:
                                pe.wait_ge(a_lo, n - 1)
                            t1_job(n - 1)
                        if u == 7 and not (first and s == 0):
                            t2_job(n - 1)
                        part = u % 4
                        if s == 0 and not last:
                            if u == 1:
                                pe.wait_ge(vt_cp, 2 * t + 1)
                                x_job(nx, 0, 0)
                            if u == 5:
                                pe.wait_ge(q_lo, CHUNKS * t + 4)
                                x_job(nx, 1, 1)
                        if s == 1 and not first:
                            if u == 0:
                                pe.wait_ge(x_lo, TILES * nx + 1) if not last else pe.wait_ge(vt_cp, 2 * t + 1)
                            if u == 4:
                                pe.wait_ge(x_lo, TILES * nx + 2) if not last else pe.wait_ge(q_lo, CHUNKS * t + 4)
                            f_part(t - 1, 1, u // 4, part)
                        if s == 2:
                            if u == 0 and not last:
                                pe.wait_ge(x_lo, TILES * nx + 1) if first else pe.wait_ge(f_add, TILES * t - 1)
                                x_job(nx, 2, 0)
                            if u == 2 and not last:
                                pe.wait_ge(x_lo, TILES * nx + 2) if first else pe.wait_ge(f_add, TILES * t)
                                x_job(nx, 3, 1)
                            if u == 4:
                                pe.wait_ge(x_lo, TILES * nx + 3) if not last else pe.wait_ge(f_add, TILES * t - 1)
                                vt_job(t, 1)
                        if s == 3 and not last:
                            if u == 0:
                                pe.wait_ge(vt_cp, 2 * t + 2)
                            if u == 4:
                                pe.wait_ge(x_lo, TILES * nx + 4)
                            q_part(nx, u // 4, part)
                        if s == 4 and not last:
                            if u < 2:
                                pe.wait_ge(q_lo, CHUNKS * nx + u + 1)
                            kv_part(nx, u % 2, u // 2)
                        if s == 5:
                            if u == 0:
                                pe.wait_ge(k_lo, nx + 1) if not last else pe.wait_ge(vt_cp, 2 * t + 2)
                            if u == 4:
                                pe.wait_ge(v_cp, nx + 1) if not last else pe.wait_ge(f_add, TILES * t)
                            f_part(t, 0, u // 4, part)
                        if s == 6 and not last:
                            if part == 0:
                                pe.wait_ge(f_add, TILES * t + u // 4 + 1)
                            q_part(nx, 2 + u // 4, part)
                        if s == 7 and u == 4 and not last:
                            pe.wait_ge(q_lo, CHUNKS * nx + 3)
                            vt_job(nx, 0)

            blocks(pe, body)
            N = STEPS * BLOCKS
            pv_unit(N - 1, 3, 1, CHUNKS - 1)
            pe.wait_ge(a_lo, N - 1)
            t1_job(N - 1)
            t2_job(N - 1)
            for qt in range(2):
                pe.wait_ge(f_add, TILES * BLOCKS - 2 - 1 + qt)
                for c in range(DC):
                    f_part(BLOCKS - 1, 1, qt, c)

            G, U, Y = bank[0:4:2], bank[1:4:2], bank[4:8]

            def x2_job(i):
                pe.wait_ge(xn2_ok, i + 1)
                if i < TILES:
                    if i == 0:
                        pe.wait_ge(f_add, TILES * BLOCKS)
                        pe.wait_ge(ot_cp, N)
                        pe.wait_ge(a_lo, N)
                elif i < 2 * TILES:
                    pe.wait_ge(x2_lo, i - TILES + 1)
                else:
                    pe.wait_ge(acc_ok, i - 2 * TILES + 1)
                for c in range(DC):
                    last = tr(Y[i % 4][:, c * P:(c + 1) * P], xn[:, i % 2, c * P:(c + 1) * P])
                last.then_inc(x2_tr, 1)

            def gate_up(k, b, par, ic, free):
                if free:
                    pe.wait_ge(hid_ok, IC * (k - 1) + ic + 1)
                tok = slice(b * BLOCK, (b + 1) * BLOCK)
                for o, bk in ((0, G[ic]), (GUW, U[ic])):
                    for c in range(DC):
                        w = slice(o + c * SC + ic * P, o + c * SC + (ic + 1) * P)
                        last = three(bk[:, :], w_h[par][:, w], w_l[par][:, w], x2T_h[:, c, tok], x2T_l[:, c, tok],
                                     c == 0, c == DC - 1)
                last.then_inc(gu_full, 1)

            def down(k, b, par, head):
                pe.wait_ge(h_lo, IC * (k + 1))
                for j in range(TILES):
                    if head and b < 3:
                        pe.wait_ge(x2_lo, TILES * (b + 1) + j + 1)
                    else:
                        pe.wait_ge(acc_ok, TILES * (k - 1) + j + 1)
                    tok = slice(j * P, (j + 1) * P)
                    for ic in range(IC):
                        w = slice(2 * GUW + ic * D, 2 * GUW + (ic + 1) * D)
                        last = three(Y[j][:, :], hT_h[:, b % 2, ic, tok], hT_l[:, b % 2, ic, tok],
                                     w_h[par][:, w], w_l[par][:, w], ic == 0, ic == IC - 1)
                    last.then_inc(y_full, 1)

            def router():
                pe.wait_ge(hid_ok, IC * BLOCKS * (SECTIONS - 2) - 1)
                pe.wait_ge(wr_ok, 2)
                for c in range(DC):
                    for part in (x2T_l, x2T_h):
                        for b in range(BLOCKS):
                            last = mm(bank[0][32 * b:32 * b + 32, :], wr[:, c, :],
                                      part[:, c, b * BLOCK:(b + 1) * BLOCK].bitcast(f32),
                                      start=c == 0 and part is x2T_l, stop=c == DC - 1 and part is x2T_h)
                last.then_inc(lg_mm, 1)
                pe.wait_ge(lg_cp, 1)
                for j in range(TILES):
                    last = tr(bank[1][:, j * P:(j + 1) * P], logT[:, j * P:(j + 1) * P])
                last.then_inc(lg_tr, 1)
                pe.wait_ge(top_ok, T // P)

            def section(sc, par):
                head = isinstance(sc, int) and sc == 0
                if isinstance(sc, int) and sc == SECTIONS - 2:
                    router()
                pe.wait_ge(w_split, sc + 1)
                for b in range(BLOCKS):
                    k = BLOCKS * sc + b
                    if head:
                        for j in range(TILES):
                            x2_job(TILES * b + j)
                        pe.wait_ge(x2_lo, TILES * (b + 1))
                    for ic in range(IC):
                        gate_up(k, b, par, ic, not (head and b == 0))
                    if not (head and b == 0):
                        down(k - 1, (b - 1) % BLOCKS, par if b else 1 - par, head)

            sections(pe, section)
            down(BLOCKS * SECTIONS - 1, BLOCKS - 1, 0, False)


_OUT = (B, S, D)


def kernel(**inputs):
    import concourse.bacc as bacc
    from concourse.bass_utils import run_bass_kernel_spmd

    def arr(name):
        return np.asarray(inputs[name])

    def rows(w):
        return np.ascontiguousarray(w.T.reshape(w.shape[1] // P, P, w.shape[0]).transpose(1, 0, 2)).reshape(P, -1)

    gate = np.concatenate([arr("L0_ffn_sh_gate"), arr("L0_ffn_r_gate")], 0)
    up = np.concatenate([arr("L0_ffn_sh_up"), arr("L0_ffn_r_up")], 0)
    down = np.concatenate([arr("L0_ffn_sh_down"), arr("L0_ffn_r_down")], 1)
    w_ffn = np.stack([
        np.concatenate([rows(gate[i * SC:(i + 1) * SC]), rows(up[i * SC:(i + 1) * SC]),
                        rows(down[:, i * SC:(i + 1) * SC])], 1) for i in range(SECTIONS)])
    ctx_t = arr("ctx_2048").reshape(BLOCKS, BLOCK, DC, P).transpose(0, 2, 3, 1)
    arrays = {
        "x": arr("x").reshape(T, D),
        "ctxT": ctx_t,
        "wq": rows(arr("L0_xattn_Wq")), "wk": rows(arr("L0_xattn_Wk")), "wv": rows(arr("L0_xattn_Wv")),
        "wfc": rows(arr("L0_xattn_Wfc")), "bfc": arr("L0_xattn_bfc"),
        "g_x": arr("g_xattn"), "g_f": arr("g_ffn"),
        "w_ffn": w_ffn, "w_r": rows(arr("L0_ffn_router_weight")),
    }
    arrays = {k: np.ascontiguousarray(v) for k, v in arrays.items()}
    nc = bacc.Bacc("TRN2", target_bir_lowering=False, num_devices=1)
    args = {k: nc.dram_tensor(k, v.shape, mybir.dt.from_np(v.dtype), kind="ExternalInput").ap()
            for k, v in arrays.items()}
    out = nc.dram_tensor("out", (T, D), mybir.dt.float32, kind="ExternalOutput").ap()
    build(nc, out=out, **args)
    r = run_bass_kernel_spmd(nc, [arrays], core_ids=[0])
    return r.results[0]["out"].reshape(_OUT)
```

```python
import numpy as np
import concourse.bass as bass
from concourse import mybir
from contextlib import ExitStack

B, S, D = 8, 256, 512
HEADS, GROUPS, DH = 32, 8, 16
SHARED, ROUTED, EXPERTS = 2048, 256, 8
P = 128
T = B * S
DC = D // P
BLOCK = 2 * S
BLOCKS = T // BLOCK
TILES = BLOCK // P
HC = P // DH
CHUNKS = HEADS // HC
STEPS = 2 * CHUNKS
RH = HEADS // GROUPS
KV = GROUPS * DH
UNITS = 8
CONSTS = 2
MROW = 64
ST = MROW + 1
VW = 32
SC = 256
SECTIONS = (SHARED + ROUTED) // SC
IC = SC // P
GUW = DC * SC
SECW = 2 * GUW + IC * D
EPS = 1e-5


def build(nc, x, ctxT, wq, wk, wv, wfc, bfc, g_x, g_f, w_ffn, w_r, out):
    f32, f32r = mybir.dt.float32, mybir.dt.float32r
    ALU, ACT, AX = mybir.AluOpType, mybir.ActivationFunctionType, mybir.AxisListType
    q_scr = nc.dram_tensor("q_scr", (2, BLOCKS, CHUNKS, P, BLOCK), f32, kind="Internal").ap()
    k_scr = nc.dram_tensor("k_scr", (2, BLOCKS, P, BLOCK), f32, kind="Internal").ap()

    with ExitStack() as ctx:
        def sem(name):
            return ctx.enter_context(nc.semaphore(name))

        def sb(name, shape, dt=f32, where=ctx):
            return where.enter_context(nc.sbuf_tensor(name, shape, dt))

        xa = sb("xa", [P, T // P, D])
        ident = sb("ident", [P, P])
        tgx = sb("tgx", [P, 1])
        tgf = sb("tgf", [P, 1])
        gates = sb("gates", [P, 2])
        mv = sb("mv", [P, 2, T // P, 2])
        rstd = sb("rstd", [P, 2, T // P])
        nmr = sb("nmr", [P, 2, T // P])
        power = sb("power", [P, T // P])
        stats = sb("stats", [P, T // P, 6])
        xn = sb("xn", [P, 4, D])
        wr_raw = sb("wr_raw", [P, DC * EXPERTS])
        wr = sb("wr", [P, DC, 32])

        att = ExitStack()
        wq_h = sb("wq_h", [P, DC, D], f32r, att)
        wq_l = sb("wq_l", [P, DC, D], f32r, att)
        wkv_h = sb("wkv_h", [P, 2, DC, KV], f32r, att)
        wkv_l = sb("wkv_l", [P, 2, DC, KV], f32r, att)
        xnT_h = sb("xnT_h", [P, DC, BLOCK], f32r, att)
        xnT_l = sb("xnT_l", [P, DC, BLOCK], f32r, att)
        cx_h = sb("cx_h", [P, 2, BLOCK], f32r, att)
        cx_l = sb("cx_l", [P, 2, BLOCK], f32r, att)
        cx_raw = sb("cx_raw", [P, 2, BLOCK], f32, att)
        wfc_h = sb("wfc_h", [P, DC, D], f32r, att)
        wfc_l = sb("wfc_l", [P, DC, D], f32r, att)
        qx_h = sb("qx_h", [P, 2, BLOCK], f32r, att)
        qx_l = sb("qx_l", [P, 2, BLOCK], f32r, att)
        kx_h = sb("kx_h", [P, BLOCK], f32r, att)
        kx_l = sb("kx_l", [P, BLOCK], f32r, att)
        vT = sb("vT", [P, BLOCK], f32, att)
        vals = sb("vals", [P, 2, S // P, GROUPS, VW], f32, att)
        q_st = sb("q_st", [P, CHUNKS, HC, S], f32r, att)
        k_st = sb("k_st", [P, 2, GROUPS, S], f32r, att)
        probs = sb("probs", [P, 4, RH, S], f32, att)
        oB = sb("oB", [P, 2 * S // VW, VW], f32, att)
        oN = sb("oN", [P, S // VW, 2 * DH], f32, att)
        aT = sb("aT", [P, S], f32, att)
        tbias = sb("tbias", [P, D], f32, att)
        mcol = sb("mcol", [P, 2, 16], f32, att)
        mT = sb("mT", [16, P], f32r, att)
        rden = sb("rden", [P, 16], f32, att)
        early = ExitStack()
        wfc_raw = sb("wfc_raw", [P, DC * D], f32, early)
        early.close()
        aT_h = sb("aT_h", [P, DC, S], f32r, att)
        aT_l = sb("aT_l", [P, DC, S], f32r, att)
        att.close()
        pflat = probs[:, :, :, :].rearrange("p a r s -> p (a r s)")
        wq_raw, wkv_raw = pflat[:, 0:DC * D], pflat[:, DC * D:DC * D + 2 * DC * KV]

        w_raw = sb("w_raw", [P, 2, SECW])
        w_h = [None, None]
        w_l = [None, None]
        w_h[0] = sb("w_h0", [P, SECW], f32r)
        w_l[0] = sb("w_l0", [P, SECW], f32r)
        w_h[1] = sb("w_h1", [P, SECW], f32r)
        w_l[1] = sb("w_l1", [P, SECW], f32r)
        x2T_h = sb("x2T_h", [P, DC, T], f32r)
        x2T_l = sb("x2T_l", [P, DC, T], f32r)
        hT_h = sb("hT_h", [P, 2, IC, BLOCK], f32r)
        hT_l = sb("hT_l", [P, 2, IC, BLOCK], f32r)
        silu = sb("silu", [P, IC, BLOCK])
        hid = sb("hid", [P, IC, BLOCK])
        logT = sb("logT", [P, BLOCK])
        top = sb("top", [P, T // P, EXPERTS])
        comb = sb("comb", [P, 4, T // P])

        bank = [ctx.enter_context(nc.psum_tensor(f"bank{i}", [P, 512], f32)) for i in range(8)]
        SMB, STB, OTB, TPB, PJ = bank[0:2], bank[2:4], bank[4], bank[5], bank[6:8]

        in_x = [sem(f"in_x{i}") for i in range(BLOCKS)]
        in_wkv, in_wq, in_wfc, in_small = sem("in_wkv"), sem("in_wq"), sem("in_wfc"), sem("in_small")
        in_cx = [sem("in_cx0"), sem("in_cx1")]
        in_w = [sem("in_w0"), sem("in_w1")]
        q_wr = [sem(f"q_wr{c}") for c in range(CHUNKS)]
        k_wr = sem("k_wr")
        q_rd = [sem(f"q_rd{c}") for c in range(CHUNKS)]
        k_rd = [sem("k_rd0"), sem("k_rd1")]
        m_rd = sem("m_rd")
        stored = sem("stored")
        consts, ident_ok, wq_ok, wkv_ok, wfc_ok = sem("consts"), sem("ident_ok"), sem("wq_ok"), sem("wkv_ok"), sem("wfc_ok")
        w_hi = sem("w_hi")
        gate_ok, tb_ok, passed = sem("gate_ok"), sem("tb_ok"), sem("passed")
        bn_one, bn_two, var_ok, rs_ok, nm_ok = sem("bn_one"), sem("bn_two"), sem("var_ok"), sem("rs_ok"), sem("nm_ok")
        cx_hi, cx_split, cx_used = sem("cx_hi"), sem("cx_split"), sem("cx_used")
        xn_ok, x_tr, x_hi, x_lo, xb_ok = sem("xn_ok"), sem("x_tr"), sem("x_hi"), sem("x_lo"), sem("xb_ok")
        q_pr, q_hi, q_lo = sem("q_pr"), sem("q_hi"), sem("q_lo")
        k_pr, k_hi, k_lo = sem("k_pr"), sem("k_hi"), sem("k_lo")
        v_cp, vt_tr, vt_cp = sem("v_cp"), sem("vt_tr"), sem("vt_cp")
        f_mm, f_add, ln2_one, ln2_ok = sem("f_mm"), sem("f_add"), sem("ln2_one"), sem("ln2_ok")
        sm_full, max_ok, zrow = sem("sm_full"), sem("max_ok"), sem("zrow")
        mt_tr, mt_cp = sem("mt_tr"), sem("mt_cp")
        st_full, exp_ok, pv_ok = sem("st_full"), sem("exp_ok"), sem("pv_ok")
        ob_ok, rden_ok, norm_ok, at_ok, a_hi, a_lo = (sem("ob_ok"), sem("rden_ok"), sem("norm_ok"), sem("at_ok"),
                                                      sem("a_hi"), sem("a_lo"))
        w_hi2, w_split, rs2_ok, nm2_ok = sem("w_hi2"), sem("w_split"), sem("rs2_ok"), sem("nm2_ok")
        xn2_ok, x2_tr, x2_hi, x2_lo = sem("xn2_ok"), sem("x2_tr"), sem("x2_hi"), sem("x2_lo")
        gu_full, silu_ok, hid_ok, h_hi, h_lo = sem("gu_full"), sem("silu_ok"), sem("hid_ok"), sem("h_hi"), sem("h_lo")
        y_full, acc_ok = sem("y_full"), sem("acc_ok")
        wr_ok, lg_mm, lg_cp, lg_tr, top_ok, comb_ok, e_ok, small = (sem("wr_ok"), sem("lg_mm"), sem("lg_cp"), sem("lg_tr"),
                                                                    sem("top_ok"), sem("comb_ok"), sem("e_ok"), sem("small"))

        block = ctx.enter_context(nc.Block())

        def blocks(eng, body):
            body(0, True, False)
            with eng.Fori(1, BLOCKS - 1) as t:
                body(t, False, False)
            body(BLOCKS - 1, False, True)

        def sections(eng, body):
            body(0, 0)
            with eng.Fori(0, (SECTIONS - 3) // 2) as i:
                body(2 * i + 1, 1)
                body(2 * i + 2, 0)
            body(SECTIONS - 2, 1)
            body(SECTIONS - 1, 0)

        @block.sync
        def _(sp):
            def r(ap):
                return ap.bitcast(f32)

            def load_cx(tb, c):
                if not (isinstance(tb, int) and tb == 0 and c < 2):
                    sp.wait_ge(cx_split, DC * tb + c - 1)
                sp.dma_start(cx_raw[:, c % 2, :], ctxT[tb, c, :, :]).then_inc(in_cx[c % 2], 16)

            def write_q(tb, oc):
                sp.wait_ge(q_hi, CHUNKS * tb + oc + 1)
                sp.wait_ge(q_lo, CHUNKS * tb + oc + 1)
                sp.dma_start(q_scr[0, tb, oc, :, :], r(qx_h[:, oc % 2, :])).then_inc(q_wr[oc], 16)
                sp.dma_start(q_scr[1, tb, oc, :, :], r(qx_l[:, oc % 2, :])).then_inc(q_wr[oc], 16)

            def read_q(tb, bb, c, n, fresh):
                if not fresh:
                    sp.wait_ge(st_full, UNITS * n)
                sp.wait_ge(q_wr[c], 32 * (tb + 1))
                for row, part in ((0, 0), (DH, 0), (2 * DH, 1)):
                    src = q_scr[part, tb, c, :, bb * S:(bb + 1) * S].rearrange("(h d) q -> d h q", d=DH)
                    sp.dma_start(r(q_st[row:row + DH, c, :, :]), src).then_inc(q_rd[c], 16)

            def write_k(tb):
                sp.wait_ge(k_hi, tb + 1)
                sp.wait_ge(k_lo, tb + 1)
                sp.dma_start(k_scr[0, tb, :, :], r(kx_h[:, :])).then_inc(k_wr, 16)
                sp.dma_start(k_scr[1, tb, :, :], r(kx_l[:, :])).then_inc(k_wr, 16)

            def read_k(tb, bb):
                sp.wait_ge(k_wr, 32 * (tb + 1))
                for row, part in ((0, 0), (DH, 1), (2 * DH, 0)):
                    src = k_scr[part, tb, :, bb * S:(bb + 1) * S].rearrange("(g d) s -> d g s", d=DH)
                    sp.dma_start(r(k_st[row:row + DH, bb, :, :]), src).then_inc(k_rd[bb], 16)

            def put_max(n, slot):
                sp.wait_ge(mt_cp, n + 1)
                for qt in range(2):
                    sp.dma_start(r(q_st[MROW:MROW + 1, slot, :, qt * P:(qt + 1) * P]),
                                 r(mT[qt * HC:(qt + 1) * HC, :])).then_inc(m_rd, 16)

            x_v = x.rearrange("(t j p) d -> t p j d", p=P, j=TILES)
            sp.dma_start(xa[:, 0:TILES, :], x_v[0]).then_inc(in_x[0], 16)
            sp.dma_start(wkv_raw[:, 0:DC * KV], wk).then_inc(in_wkv, 16)
            sp.dma_start(wkv_raw[:, DC * KV:2 * DC * KV], wv).then_inc(in_wkv, 16)
            load_cx(0, 0)
            load_cx(0, 1)
            sp.dma_start(wq_raw, wq).then_inc(in_wq, 16)
            load_cx(0, 2)
            load_cx(0, 3)
            sp.dma_start(tbias[:, :], bfc.partition_broadcast(P)).then_inc(in_small, 16)
            sp.dma_start(gates[:, 0:1], g_x.partition_broadcast(P)).then_inc(in_small, 16)
            sp.dma_start(gates[:, 1:2], g_f.partition_broadcast(P)).then_inc(in_small, 16)
            sp.dma_start(wr_raw[:, :], w_r).then_inc(in_small, 16)
            for t in range(1, BLOCKS):
                sp.dma_start(xa[:, TILES * t:TILES * (t + 1), :], x_v[t]).then_inc(in_x[t], 16)
            sp.dma_start(wfc_raw[:, :], wfc).then_inc(in_wfc, 16)
            sp.wait_ge(consts, CONSTS)
            write_k(0)
            read_k(0, 0)
            for c in range(CHUNKS):
                write_q(0, c)
                if c < 3:
                    read_q(0, 0, c, 0, True)
            put_max(0, 0)

            def body(t, first, last):
                for s in range(STEPS):
                    n = STEPS * t + s
                    if s == 0:
                        if not first:
                            sp.wait_ge(st_full, UNITS * n)
                        read_k(t, 1)
                    if s + 3 < STEPS or not last and s != 6:
                        e = s + 3
                        tb = t if e < STEPS else t + 1
                        read_q(tb, e % STEPS // CHUNKS, e % CHUNKS, n, first and s == 0)
                    if s in (0, 2) and not last:
                        load_cx(t + 1, s)
                        load_cx(t + 1, s + 1)
                    if not last:
                        if s == 4:
                            write_k(t + 1)
                        if s == 6:
                            write_q(t + 1, 1)
                    if not last or s + 1 < STEPS:
                        put_max(n + 1, (s + 1) % CHUNKS)
                    if not last:
                        if s == 3:
                            write_q(t + 1, 0)
                        if s == 4:
                            read_k(t + 1, 0)
                        if s == 6:
                            read_q(t + 1, 0, 1, n, False)
                            write_q(t + 1, 2)
                        if s == 7:
                            write_q(t + 1, 3)
                    elif s == 0:
                        sp.wait_ge(q_lo, CHUNKS * BLOCKS)
                        sp.wait_ge(k_lo, BLOCKS)
                        sp.wait_ge(v_cp, BLOCKS)
                        for sc in range(2):
                            sp.dma_start(w_raw[:, sc, :], w_ffn[sc, :, :]).then_inc(in_w[sc], 16)

            blocks(sp, body)

            def section(sc, par):
                if isinstance(sc, int) and sc + 2 >= SECTIONS:
                    return
                sp.wait_ge(w_split, sc + 1)
                sp.dma_start(w_raw[:, par, :], w_ffn[sc + 2, :, :]).then_inc(in_w[par], 16)

            body_n = SECTIONS - 2
            section(0, 0)
            with sp.Fori(0, (body_n - 1) // 2) as i:
                section(2 * i + 1, 1)
                section(2 * i + 2, 0)
            o_v = out.rearrange("(i p) d -> i p d", p=P)
            for i in range(T // P):
                sp.wait_ge(acc_ok, TILES * BLOCKS * (SECTIONS - 1) + i + 1)
                sp.dma_start(o_v[i], xa[:, i, :]).then_inc(stored, 16)
            sp.wait_ge(stored, 16 * (T // P))

        @block.gpsimd
        def _(pool):
            g = nc.gpsimd

            def cx_low(tb, c):
                pool.wait_ge(cx_hi, DC * tb + c + 1)
                g.tensor_tensor(cx_l[:, c % 2, :], cx_raw[:, c % 2, :], cx_h[:, c % 2, :].bitcast(f32),
                                ALU.subtract).then_inc(cx_split, 1)

            def root(lot, a, b):
                g.tensor_scalar(rstd[:, lot, a:b], mv[:, lot, a:b, 1], EPS, 0.0, ALU.add, ALU.add).then_inc(var_ok, 1)

            g.memset(ident[:, :], 0.0).then_inc(small, 1)
            pool.wait_ge(small, 1)
            g.affine_select(out=ident[:, :], in_=ident[:, :], compare_op=ALU.not_equal, fill=1.0, base=0,
                            pattern=[[-1, P]], channel_multiplier=1).then_inc(ident_ok, 1)
            g.memset(power[:, :], -0.5)
            g.memset(vals[:, :, :, :, DH:VW], 1.0).then_inc(small, 1)
            pool.wait_ge(small, 2)
            g.memset(q_st[0:ST, :, :, :].bitcast(f32), 0.0).then_inc(consts, 1)
            for lot, (a, b) in enumerate(((0, TILES), (TILES, T // P))):
                pool.wait_ge(bn_two, b)
                root(0, a, b)
                pool.wait_ge(var_ok, lot + 1)
                g.tensor_tensor(rstd[:, 0, a:b], rstd[:, 0, a:b], power[:, 0:b - a], ALU.pow).then_inc(rs_ok, 1)

            def add_bias(tb):
                pool.wait_ge(tb_ok, 1)
                for j in range(TILES):
                    pool.wait_ge(xn_ok, TILES * tb + j + 1)
                    tile = xa[:, bass.ds(TILES * tb + j, 1), :].rearrange("p a d -> p (a d)")
                    g.tensor_tensor(tile, tile, tbias[:, :], ALU.add).then_inc(xb_ok, 1)
                pool.wait_ge(xb_ok, TILES * (tb + 1))

            add_bias(0)

            def body(t, first, last):
                for s in range(STEPS):
                    n = STEPS * t + s
                    if not last or s + 3 < STEPS:
                        if not (first and s == 0):
                            pool.wait_ge(st_full, UNITS * n)
                        pool.sem_inc(passed)
                        g.memset(q_st[MROW:ST, (s + 3) % CHUNKS, :, :].bitcast(f32), 0.0).then_inc(zrow, 1)
                        pool.wait_ge(zrow, n + 1)
                    if last:
                        continue
                    if s in (1, 3):
                        cx_low(t + 1, s - 1)
                        cx_low(t + 1, s)
                        pool.wait_ge(cx_split, DC * (t + 1) + s + 1)
                    if s == 4:
                        add_bias(t + 1)
                if last:
                    split_w(0, 0)

            def split_w(sc, par):
                pool.wait_ge(in_w[par], 8 * (sc - par) + 16)
                if isinstance(sc, int) and sc == 0:
                    pool.wait_ge(q_lo, CHUNKS * BLOCKS)
                    pool.wait_ge(v_cp, BLOCKS)
                if isinstance(sc, int) and sc == 1:
                    pool.wait_ge(f_add, TILES * BLOCKS)
                    pool.wait_ge(a_lo, STEPS * BLOCKS)
                if not isinstance(sc, int) or sc >= 2:
                    pool.wait_ge(y_full, TILES * BLOCKS * (sc - 1))
                pool.sem_inc(passed)
                g.tensor_copy(w_h[par][:, :], w_raw[:, par, :]).then_inc(w_hi2, 1)
                pool.wait_ge(w_hi2, sc + 1)
                g.tensor_tensor(w_l[par][:, :], w_raw[:, par, :], w_h[par][:, :].bitcast(f32),
                                ALU.subtract).then_inc(w_split, 1)

            blocks(pool, body)
            for lot, (a, b) in enumerate(((0, 12), (12, 16))):
                pool.wait_ge(ln2_ok, b)
                root(1, a, b)
                pool.wait_ge(var_ok, lot + 3)
                g.tensor_tensor(rstd[:, 1, a:b], rstd[:, 1, a:b], power[:, 0:b - a], ALU.pow).then_inc(rs2_ok, 1)
            split_w(1, 1)
            with pool.Fori(0, (SECTIONS - 3) // 2) as i:
                split_w(2 * i + 2, 0)
                split_w(2 * i + 3, 1)
            split_w(SECTIONS - 1, 0)

        @block.scalar
        def _(act):
            def copy(out, in_):
                return nc.scalar.activation(out, in_, ACT.Copy)

            def normalise(lot, i, slot):
                tile = xa[:, bass.ds(i, 1), :].rearrange("p a d -> p (a d)")
                return nc.scalar.activation(xn[:, slot, :], tile, ACT.Identity,
                                            bias=nmr[:, lot, bass.ds(i, 1)], scale=rstd[:, lot, bass.ds(i, 1)])

            def xn_tile(tb, j):
                if not (isinstance(tb, int) and tb == 0):
                    act.wait_ge(x_tr, TILES * (tb - 1) + j + 1)
                normalise(0, TILES * tb + j, j).then_inc(xn_ok, 1)

            def cx_high(tb, c):
                act.wait_ge(in_cx[c % 2], 16 * (2 * tb + c // 2 + 1))
                if not (isinstance(tb, int) and tb == 0 and c < 2):
                    act.wait_ge(cx_used, DC * tb + c - 1)
                copy(cx_h[:, c % 2, :], cx_raw[:, c % 2, :]).then_inc(cx_hi, 1)

            def x_high(tb, j):
                act.wait_ge(x_tr, TILES * tb + j + 1)
                if not (isinstance(tb, int) and tb == 0):
                    act.wait_ge(q_pr, CHUNKS * tb)
                copy(xnT_h[:, :, j * P:(j + 1) * P], PJ[j % 2][:, :].rearrange("p (c q) -> p c q", c=DC)).then_inc(x_hi, 1)

            def q_high(tb, oc):
                act.wait_ge(q_pr, CHUNKS * tb + oc + 1)
                if isinstance(tb, int) and tb == 0:
                    if oc >= 2:
                        act.wait_ge(q_wr[oc - 2], 32)
                else:
                    act.wait_ge(q_wr[(oc + 2) % 4], 32 * (tb + 1) if oc >= 2 else 32 * tb)
                copy(qx_h[:, oc % 2, :], PJ[(oc + 1) % 2][:, :]).then_inc(q_hi, 1)

            def k_high(tb):
                act.wait_ge(k_pr, tb + 1)
                if not (isinstance(tb, int) and tb == 0):
                    act.wait_ge(k_wr, 32 * tb)
                copy(kx_h[:, :], PJ[0][:, :]).then_inc(k_hi, 1)

            def v_copy(tb):
                act.wait_ge(cx_used, DC * (tb + 1))
                if not (isinstance(tb, int) and tb == 0):
                    act.wait_ge(vt_tr, 2 * tb)
                copy(vT[:, :], PJ[1][:, :]).then_inc(v_cp, 1)

            def vt_copy(tb, bb):
                act.wait_ge(vt_tr, 2 * tb + bb + 1)
                if not (isinstance(tb, int) and tb == 0):
                    act.wait_ge(pv_ok, 4 * (STEPS * (tb - 1) + CHUNKS * (bb + 1)))
                copy(vals[:, bb, :, :, 0:DH],
                     PJ[(bb + 1) % 2][:, 0:S].rearrange("p (k g d) -> p k g d", k=S // P, g=GROUPS)).then_inc(vt_cp, 1)

            act.wait_ge(in_wkv, 32)
            copy(wkv_h[:, :, :, :].rearrange("p a c n -> p (a c n)"), wkv_raw).then_inc(w_hi, 1)
            cx_high(0, 0)
            cx_high(0, 1)
            act.wait_ge(nm_ok, 1)
            xn_tile(0, 0)
            xn_tile(0, 1)
            cx_high(0, 2)
            xn_tile(0, 2)
            cx_high(0, 3)
            xn_tile(0, 3)
            act.wait_ge(in_wq, 16)
            copy(wq_h[:, :, :].rearrange("p c n -> p (c n)"), wq_raw).then_inc(w_hi, 1)
            k_high(0)
            v_copy(0)
            for j in range(TILES):
                x_high(0, j)
            act.wait_ge(in_small, 64)
            nc.scalar.activation(tgx[:, :], gates[:, 0:1], ACT.Tanh).then_inc(gate_ok, 1)
            nc.scalar.activation(tgf[:, :], gates[:, 1:2], ACT.Tanh).then_inc(gate_ok, 1)
            q_high(0, 0)
            q_high(0, 1)
            act.wait_ge(in_wfc, 16)
            copy(wfc_h[:, :, :].rearrange("p c n -> p (c n)"), wfc_raw[:, :]).then_inc(w_hi, 1)
            q_high(0, 2)
            q_high(0, 3)
            vt_copy(0, 0)
            act.wait_ge(nm_ok, 2)
            act.wait_ge(wfc_ok, 1)
            act.wait_ge(wq_ok, 1)
            act.wait_ge(wkv_ok, 1)

            def a_high(n, c, batch):
                act.wait_ge(at_ok, n + 1)
                if not (isinstance(batch, int) and batch == 0):
                    act.wait_ge(f_mm, 2 * batch)
                copy(aT_h[:, c, :], aT[:, :]).then_inc(a_hi, 1)

            def body(t, first, last):
                nx = t + 1
                for s in range(STEPS):
                    n = STEPS * t + s
                    for u in range(UNITS):
                        p = u // 2
                        act.wait_ge(st_full, UNITS * n + u + 1)
                        if u % 2 == 0 and not (first and s == 0):
                            act.wait_ge(pv_ok, 4 * (n - 1) + p + 1)
                        nc.scalar.activation(probs[:, p, 2 * (u % 2):2 * (u % 2) + 2, :],
                                             STB[u % 2][:, :].rearrange("p (r q) -> p r q", r=2),
                                             ACT.Exp, scale=float(DH) ** -0.5).then_inc(exp_ok, 1)
                        if u == 4 and not (first and s == 0):
                            a_high(n - 1, (s - 1) % CHUNKS, 2 * t + (s - 1) // CHUNKS)
                        if s == 2 and u == 2:
                            vt_copy(t, 1)
                        if last:
                            continue
                        if s == 0 and u < 2:
                            xn_tile(nx, u)
                        if s == 0 and u in (2, 4):
                            x_high(nx, u // 2 - 1)
                        if s == 1 and u in (1, 3):
                            xn_tile(nx, 2 + u // 2)
                        if s == 1 and u in (2, 6):
                            cx_high(nx, u // 4)
                        if s == 1 and u in (5, 7):
                            x_high(nx, u // 2)
                        if s == 3 and u == 0:
                            q_high(nx, 0)
                        if s == 3 and u in (2, 4):
                            cx_high(nx, 1 + u // 2)
                        if s == 4 and u == 0:
                            k_high(nx)
                        if s == 4 and u == 4:
                            v_copy(nx)
                        if s == 6 and u == 0:
                            q_high(nx, 1)
                        if s == 6 and u == 4:
                            q_high(nx, 2)
                        if s == 7 and u == 4:
                            q_high(nx, 3)
                        if s == 7 and u == 6:
                            vt_copy(nx, 0)

            blocks(act, body)
            a_high(STEPS * BLOCKS - 1, CHUNKS - 1, B - 1)

            def x2_tile(i):
                if i == 0 or i == 12:
                    act.wait_ge(nm2_ok, 1 if i == 0 else 2)
                if i >= 4:
                    act.wait_ge(x2_tr, i - 3)
                normalise(1, i, i % 4).then_inc(xn2_ok, 1)

            def x2_high(i):
                act.wait_ge(x2_tr, i + 1)
                copy(x2T_h[:, :, i * P:(i + 1) * P],
                     bank[4 + i % 4][:, :].rearrange("p (c q) -> p c q", c=DC)).then_inc(x2_hi, 1)

            def section(sc, par):
                head = isinstance(sc, int) and sc == 0
                if isinstance(sc, int) and sc == SECTIONS - 1:
                    act.wait_ge(top_ok, T // P)
                    act.wait_ge(comb_ok, 1)
                    nc.scalar.activation(comb[:, 1, :], comb[:, 0, :], ACT.Exp).then_inc(e_ok, 1)
                for b in range(BLOCKS):
                    k = BLOCKS * sc + b
                    if head:
                        x2_tile(TILES * b)
                        x2_tile(TILES * b + 1)
                        for j in range(TILES):
                            x2_high(TILES * b + j)
                            if j < 2:
                                x2_tile(TILES * b + j + 2)
                    for ic in range(IC):
                        act.wait_ge(gu_full, IC * k + ic + 1)
                        if not (head and b == 0):
                            act.wait_ge(hid_ok, IC * (k - 1) + ic + 1)
                        nc.scalar.activation(silu[:, ic, :], bank[2 * ic][:, :], ACT.Silu).then_inc(silu_ok, 1)
                    for ic in range(IC):
                        act.wait_ge(hid_ok, IC * k + ic + 1)
                        if not (head and b < 2):
                            act.wait_ge(y_full, TILES * (k - 1))
                        copy(hT_h[:, b % 2, ic, :], hid[:, ic, :]).then_inc(h_hi, 1)

            sections(act, section)

        @block.vector
        def _(dve):
            v = nc.vector

            def low(out, psum, high):
                return v.tensor_tensor(out, psum, high.bitcast(f32), ALU.subtract)

            def aggregate(lot, i, done):
                v.bn_aggr(mv[:, lot, i, :], stats[:, i, :]).then_inc(done, 1)

            def x_low(tb, j):
                dve.wait_ge(x_hi, TILES * tb + j + 1)
                sl = slice(j * P, (j + 1) * P)
                low(xnT_l[:, :, sl], PJ[j % 2][:, :].rearrange("p (c q) -> p c q", c=DC), xnT_h[:, :, sl]).then_inc(x_lo, 1)

            def q_low(tb, oc):
                dve.wait_ge(q_hi, CHUNKS * tb + oc + 1)
                low(qx_l[:, oc % 2, :], PJ[(oc + 1) % 2][:, :], qx_h[:, oc % 2, :]).then_inc(q_lo, 1)

            def k_low(tb):
                dve.wait_ge(k_hi, tb + 1)
                low(kx_l[:, :], PJ[0][:, :], kx_h[:, :]).then_inc(k_lo, 1)

            def maximum(n, u, par):
                qt, g2, half = u // 2 % 2, u // 4, u % 2
                dve.wait_ge(sm_full, UNITS * n + u + 1)
                if u == 0 and not (isinstance(n, int) and n < 2):
                    dve.wait_ge(mt_tr, n - 1)
                at = qt * HC + g2 * RH + half * 2
                v.tensor_reduce(mcol[:, par, at:at + 2], SMB[u % 2][:, :].rearrange("p (r k) -> p r k", r=2),
                                AX.X, ALU.max).then_inc(max_ok, 1)

            def m_copy(n):
                dve.wait_ge(mt_tr, n + 1)
                if not (isinstance(n, int) and n == 0):
                    dve.wait_ge(m_rd, 32 * n)
                v.tensor_scalar(mT[:, :], TPB[0:16, 0:P], -1.0, None, ALU.mult).then_inc(mt_cp, 1)

            def f_done(t, bb, qt):
                f = TILES * t + 2 * bb + qt
                dve.wait_ge(f_mm, f + 1)
                dve.wait_ge(xb_ok, f + 1)
                tile = xa[:, bass.ds(f, 1), :].rearrange("p a d -> p (a d)")
                v.scalar_tensor_tensor(tile, PJ[qt][:, :], tgx[:, :], tile, ALU.mult, ALU.add).then_inc(f_add, 1)
                dve.wait_ge(f_add, f + 1)
                dve.wait_ge(bn_two, T // P)
                v.bn_stats(stats[:, bass.ds(f, 1), :].rearrange("p a k -> p (a k)"), tile).then_inc(ln2_one, 1)

            def norm_rows(lot, a, b):
                dve.wait_ge(rs_ok, lot + 1)
                v.scalar_tensor_tensor(nmr[:, 0, a:b], mv[:, 0, a:b, 0], -1.0, rstd[:, 0, a:b],
                                       ALU.mult, ALU.mult).then_inc(nm_ok, 1)

            def statistics(t):
                dve.wait_ge(in_x[t], 16)
                for i in range(TILES * t, TILES * (t + 1)):
                    v.bn_stats(stats[:, i, :], xa[:, i, :]).then_inc(bn_one, 1)
                dve.wait_ge(bn_one, TILES * (t + 1))
                for i in range(TILES * t, TILES * (t + 1)):
                    aggregate(0, i, bn_two)

            def cx_low(c):
                dve.wait_ge(cx_hi, c + 1)
                low(cx_l[:, c % 2, :], cx_raw[:, c % 2, :], cx_h[:, c % 2, :]).then_inc(cx_split, 1)

            v.memset(k_st[0:ST, :, :, :].bitcast(f32), 1.0).then_inc(consts, 1)
            statistics(0)
            dve.wait_ge(w_hi, 1)
            v.tensor_tensor(wkv_l[:, :, :, :].rearrange("p a c n -> p (a c n)"), wkv_raw,
                            wkv_h[:, :, :, :].rearrange("p a c n -> p (a c n)").bitcast(f32), ALU.subtract).then_inc(wkv_ok, 1)
            cx_low(0)
            cx_low(1)
            norm_rows(0, 0, TILES)
            cx_low(2)
            cx_low(3)
            dve.wait_ge(w_hi, 2)
            v.tensor_tensor(wq_l[:, :, :].rearrange("p c n -> p (c n)"), wq_raw,
                            wq_h[:, :, :].rearrange("p c n -> p (c n)").bitcast(f32),
                            ALU.subtract).then_inc(wq_ok, 1)
            k_low(0)
            for j in range(TILES):
                x_low(0, j)
            statistics(1)
            q_low(0, 0)
            dve.wait_ge(gate_ok, 2)
            v.tensor_scalar(tbias[:, :], tbias[:, :], tgx[:, :], None, ALU.mult).then_inc(tb_ok, 1)
            q_low(0, 1)
            statistics(2)
            q_low(0, 2)
            dve.wait_ge(w_hi, 3)
            v.tensor_tensor(wfc_l[:, :, :].rearrange("p c n -> p (c n)"), wfc_raw[:, :],
                            wfc_h[:, :, :].rearrange("p c n -> p (c n)").bitcast(f32),
                            ALU.subtract).then_inc(wfc_ok, 1)
            for u in range(UNITS):
                maximum(0, u, 0)
            q_low(0, 3)
            m_copy(0)
            statistics(3)
            for u in range(UNITS):
                maximum(1, u, 1)
            norm_rows(1, TILES, T // P)
            v.memset(wr[:, :, :], 0.0).then_inc(wr_ok, 1)
            dve.wait_ge(wr_ok, 1)
            v.tensor_copy(wr[:, :, 0:EXPERTS], wr_raw[:, :].rearrange("p (c e) -> p c e", c=DC)).then_inc(wr_ok, 1)

            def a_low(n, c):
                dve.wait_ge(a_hi, n + 1)
                low(aT_l[:, c, :], aT[:, :], aT_h[:, c, :]).then_inc(a_lo, 1)

            def o_turn(n):
                dve.wait_ge(pv_ok, 4 * n + 4)
                v.transpose(oB[:, :, :].rearrange("p b w -> p (b w)"), OTB[:, :]).then_inc(ob_ok, 1)

            def inverse(n):
                dve.wait_ge(ob_ok, n + 1)
                v.reciprocal(rden[:, :], oB[:, :, DH]).then_inc(rden_ok, 1)

            def divide(n):
                dve.wait_ge(rden_ok, n + 1)
                v.tensor_tensor(oN[:, :, :].rearrange("p b (g d) -> p g b d", g=2),
                                oB[:, :, 0:DH].rearrange("p (g b) d -> p g b d", g=2),
                                rden[:, :].rearrange("p (g b) -> p g b", g=2).unsqueeze(3).to_broadcast([P, 2, S // VW, DH]),
                                ALU.mult).then_inc(norm_ok, 1)
                dve.wait_ge(norm_ok, n + 1)
                if not (isinstance(n, int) and n == 0):
                    dve.wait_ge(a_lo, n)
                v.transpose(aT[:, :], oN[:, :, :].rearrange("p b w -> p (b w)")).then_inc(at_ok, 1)

            def body(t, first, last):
                nx = t + 1
                for s in range(STEPS):
                    n = STEPS * t + s
                    prev = not (first and s == 0)
                    for u in range(UNITS):
                        if not last or s + 2 < STEPS:
                            maximum(n + 2, u, s % 2)
                        if not last and s == 3 and u == 1:
                            q_low(nx, 0)
                        if prev:
                            if u == 1:
                                o_turn(n - 1)
                            if u == 2:
                                inverse(n - 1)
                            if u == 3:
                                divide(n - 1)
                            if u == 5:
                                a_low(n - 1, (s - 1) % CHUNKS)
                        if u == 2 and (not last or s + 1 < STEPS):
                            m_copy(n + 1)
                        if s == 1 and u in (0, 5) and not first:
                            f_done(t - 1, 1, u // 5)
                        if s == 5 and u in (0, 5):
                            f_done(t, 0, u // 5)
                        if last:
                            continue
                        if s == 0 and u in (3, 5):
                            x_low(nx, u // 2 - 1)
                        if s == 1 and u == 6:
                            x_low(nx, 2)
                        if s == 2 and u == 0:
                            x_low(nx, 3)
                        if s == 4 and u == 1:
                            k_low(nx)
                        if s == 6 and u in (1, 6):
                            q_low(nx, 1 + u // 6)
                        if s == 7 and u == 6:
                            q_low(nx, 3)
                    if last and s == 3:
                        dve.wait_ge(ln2_one, TILES * t)
                        for i in range(TILES * t):
                            aggregate(1, i, ln2_ok)

            blocks(dve, body)
            N = STEPS * BLOCKS
            o_turn(N - 1)
            inverse(N - 1)
            divide(N - 1)
            a_low(N - 1, CHUNKS - 1)
            for i, (a, b) in enumerate(((0, 12), (12, 16))):
                if i:
                    f_done(BLOCKS - 1, 1, 0)
                    f_done(BLOCKS - 1, 1, 1)
                    dve.wait_ge(ln2_one, T // P)
                    for i2 in range(a, b):
                        aggregate(1, i2, ln2_ok)
                dve.wait_ge(rs2_ok, i + 1)
                v.scalar_tensor_tensor(nmr[:, 1, a:b], mv[:, 1, a:b, 0], -1.0, rstd[:, 1, a:b],
                                       ALU.mult, ALU.mult).then_inc(nm2_ok, 1)

            def x2_low(i):
                sl = slice(i * P, (i + 1) * P)
                dve.wait_ge(x2_hi, i + 1)
                low(x2T_l[:, :, sl], bank[4 + i % 4][:, :].rearrange("p (c q) -> p c q", c=DC),
                    x2T_h[:, :, sl]).then_inc(x2_lo, 1)

            def accumulate(k, b, routed):
                for j in range(TILES):
                    i = TILES * b + j
                    dve.wait_ge(y_full, TILES * k + j + 1)
                    scale = comb[:, 0, i:i + 1] if routed else tgf[:, :]
                    v.scalar_tensor_tensor(xa[:, i, :], bank[4 + j][:, :], scale, xa[:, i, :],
                                           ALU.mult, ALU.add).then_inc(acc_ok, 1)

            def router():
                dve.wait_ge(lg_mm, 1)
                v.tensor_copy(logT[:, :], bank[0][:, :]).then_inc(lg_cp, 1)
                dve.wait_ge(lg_tr, 1)
                lg = bank[1][:, :].rearrange("p (j b e) -> p j b e", j=TILES, b=BLOCKS)
                for b in range(BLOCKS):
                    for j in range(TILES):
                        v.max(top[:, TILES * b + j, :], lg[:, j, b, 0:EXPERTS]).then_inc(top_ok, 1)
                dve.wait_ge(top_ok, T // P)
                v.tensor_tensor(comb[:, 0, :], top[:, :, 1], top[:, :, 0], ALU.subtract).then_inc(comb_ok, 1)

            def weights():
                dve.wait_ge(e_ok, 1)
                v.tensor_scalar(comb[:, 2, :], comb[:, 1, :], 1.0, None, ALU.add).then_inc(comb_ok, 1)
                dve.wait_ge(comb_ok, 2)
                v.reciprocal(comb[:, 3, :], comb[:, 2, :]).then_inc(comb_ok, 1)
                dve.wait_ge(comb_ok, 3)
                v.tensor_tensor(comb[:, 1, :], comb[:, 1, :], comb[:, 3, :], ALU.mult).then_inc(comb_ok, 1)
                dve.wait_ge(comb_ok, 4)
                v.tensor_tensor(comb[:, 2, :], comb[:, 1, :], comb[:, 3, :], ALU.add).then_inc(comb_ok, 1)
                dve.wait_ge(comb_ok, 5)
                v.tensor_scalar(comb[:, 0, :], comb[:, 2, :], tgf[:, :], None, ALU.mult).then_inc(comb_ok, 1)
                dve.wait_ge(comb_ok, 6)

            def section(sc, par):
                head = isinstance(sc, int) and sc == 0
                tail = isinstance(sc, int) and sc == SECTIONS - 1
                if isinstance(sc, int) and sc == SECTIONS - 2:
                    router()
                for b in range(BLOCKS):
                    k = BLOCKS * sc + b
                    if head:
                        for j in range(TILES):
                            x2_low(TILES * b + j)
                    for ic in range(IC):
                        dve.wait_ge(silu_ok, IC * k + ic + 1)
                        if not (head and b == 0):
                            dve.wait_ge(h_lo, IC * (k - 1) + ic + 1)
                        v.tensor_tensor(hid[:, ic, :], bank[2 * ic + 1][:, :], silu[:, ic, :], ALU.mult).then_inc(hid_ok, 1)
                    for ic in range(IC):
                        dve.wait_ge(h_hi, IC * k + ic + 1)
                        v.tensor_tensor(hT_l[:, b % 2, ic, :], hid[:, ic, :], hT_h[:, b % 2, ic, :].bitcast(f32),
                                        ALU.subtract).then_inc(h_lo, 1)
                    if not (head and b == 0):
                        accumulate(k - 1, (b - 1) % BLOCKS, tail and b > 0)
                if tail:
                    accumulate(BLOCKS * SECTIONS - 1, BLOCKS - 1, True)

            def section_w(sc, par):
                if isinstance(sc, int) and sc == SECTIONS - 1:
                    weights()
                section(sc, par)

            sections(dve, section_w)

        @block.tensor
        def _(pe):
            mm = nc.tensor.matmul

            def three(out, a_h, a_l, b_h, b_l, start, stop):
                mm(out, a_h, b_l, start=start, stop=False)
                mm(out, a_l, b_h, start=False, stop=False)
                return mm(out, a_h, b_h, start=False, stop=stop)

            def tr(out, in_):
                return nc.tensor.transpose(out, in_, ident[:, :])

            def x_job(tb, j):
                pe.wait_ge(xn_ok, TILES * tb + j + 1)
                for c in range(DC):
                    last = tr(PJ[j % 2][:, c * P:(c + 1) * P], xn[:, j, c * P:(c + 1) * P])
                last.then_inc(x_tr, 1)

            def q_part(tb, oc, c):
                if c == 0:
                    pe.wait_ge(x_lo, TILES * (tb + 1))
                w = slice(oc * P, (oc + 1) * P)
                last = three(PJ[(oc + 1) % 2][:, :], wq_h[:, c, w], wq_l[:, c, w], xnT_h[:, c, :], xnT_l[:, c, :],
                             c == 0, c == DC - 1)
                if c == DC - 1:
                    last.then_inc(q_pr, 1)

            def kv_part(tb, a, c):
                pe.wait_ge(cx_split, DC * tb + c + 1)
                last = three(PJ[a][:, :], wkv_h[:, a, c, :], wkv_l[:, a, c, :], cx_h[:, c % 2, :], cx_l[:, c % 2, :],
                             c == 0, c == DC - 1)
                if a == 1:
                    last.then_inc(cx_used, 1)
                elif c == DC - 1:
                    last.then_inc(k_pr, 1)

            def vt_job(tb, bb):
                pe.wait_ge(v_cp, tb + 1)
                for kt in range(S // P):
                    last = tr(PJ[(bb + 1) % 2][:, kt * P:(kt + 1) * P], vT[:, bb * S + kt * P:bb * S + (kt + 1) * P])
                last.then_inc(vt_tr, 1)

            def f_part(t, bb, qt, c):
                if qt == 0:
                    pe.wait_ge(a_lo, STEPS * t + CHUNKS * bb + c + 1)
                w = slice(qt * P, (qt + 1) * P)
                last = three(PJ[qt][:, :], aT_h[:, c, w], aT_l[:, c, w], wfc_h[:, c, :], wfc_l[:, c, :],
                             c == 0, c == DC - 1)
                if c == DC - 1:
                    last.then_inc(f_mm, 1)

            def sm_unit(n, u, bb, c):
                qt, g2, half = u // 2 % 2, u // 4, u % 2
                if not (isinstance(n, int) and n == 0 and u < 2):
                    pe.wait_ge(max_ok, UNITS * n + u - 1)
                for j in range(2):
                    last = mm(SMB[u % 2][:, j * S:(j + 1) * S], q_st[0:ST, c, g2 * RH + half * 2 + j, qt * P:(qt + 1) * P],
                              k_st[0:ST, bb, 2 * c + g2, :], start=True, stop=True)
                last.then_inc(sm_full, 1)

            def st_unit(n, u, bb, c):
                g2, kt, half = u // 4, u // 2 % 2, u % 2
                if not (isinstance(n, int) and n == 0 and u < 2):
                    pe.wait_ge(exp_ok, UNITS * n + u - 1)
                h = g2 * RH + half * 2
                mm(STB[u % 2][:, :], k_st[0:ST, bb, 2 * c + g2, kt * P:(kt + 1) * P], q_st[0:ST, c, h:h + 2, :],
                   start=True, stop=True).then_inc(st_full, 1)

            def pv_unit(n, p, bb, c):
                g2, kt = p // 2, p % 2
                pe.wait_ge(exp_ok, UNITS * n + 2 * p + 2)
                if p == 0 and not (isinstance(n, int) and n == 0):
                    pe.wait_ge(ob_ok, n)
                for r in range(RH):
                    last = mm(OTB[32 * r:32 * r + VW, g2 * S:(g2 + 1) * S], vals[:, bb, kt, 2 * c + g2, :],
                              probs[:, p, r, :], start=kt == 0, stop=kt == 1)
                last.then_inc(pv_ok, 1)

            def mt_job(n, par):
                pe.wait_ge(max_ok, UNITS * n + UNITS)
                tr(TPB[0:16, 0:P], mcol[:, par, :]).then_inc(mt_tr, 1)

            pe.wait_ge(ident_ok, 1)
            pe.wait_ge(wkv_ok, 1)
            for c in range(DC):
                kv_part(0, 0, c)
                kv_part(0, 1, c)
            for j, (done, count) in enumerate(((k_lo, 1), (v_cp, 1), (x_lo, 1), (x_lo, 2))):
                pe.wait_ge(done, count)
                x_job(0, j)
            pe.wait_ge(wq_ok, 1)

            def q_job(oc):
                if oc >= 2:
                    pe.wait_ge(q_lo, oc - 1)
                for c in range(DC):
                    q_part(0, oc, c)

            def maxima(n):
                pe.wait_ge(q_rd[n], 48)
                for u in range(UNITS):
                    sm_unit(n, u, 0, n)

            for oc in range(3):
                q_job(oc)
            pe.wait_ge(consts, CONSTS)
            pe.wait_ge(k_rd[0], 48)
            maxima(0)
            q_job(3)
            pe.wait_ge(q_lo, 3)
            vt_job(0, 0)
            mt_job(0, 0)
            maxima(1)
            pe.wait_ge(wfc_ok, 1)

            def body(t, first, last):
                nx = t + 1
                for s in range(STEPS):
                    n = STEPS * t + s
                    bb, c = s // CHUNKS, s % CHUNKS
                    e = s + 2
                    te = t if e < STEPS else nx
                    be, ce = e % STEPS // CHUNKS, e % CHUNKS
                    look = not last or e < STEPS
                    for u in range(UNITS):
                        if look:
                            if u == 0:
                                pe.wait_ge(q_rd[ce], 48 * (2 * te + be + 1))
                                pe.wait_ge(k_rd[be], 48 * (te + 1))
                                if not (first and s == 0):
                                    pe.wait_ge(zrow, n)
                            sm_unit(n + 2, u, be, ce)
                        if u == 0:
                            pe.wait_ge(m_rd, 32 * (n + 1))
                        st_unit(n, u, bb, c)
                        if u == 1 and not (first and s == 0):
                            pv_unit(n - 1, 3, (s - 1) % STEPS // CHUNKS, (s - 1) % CHUNKS)
                        if u == 3 and c == 0:
                            pe.wait_ge(vt_cp, 2 * t + bb + 1)
                        if u in (3, 5, 7):
                            pv_unit(n, u // 2 - 1, bb, c)
                        if u == 2 and (not last or s + 1 < STEPS):
                            pe.wait_ge(mt_cp, n + 1)
                            mt_job(n + 1, (s + 1) % 2)
                        part = u % 4
                        if s == 0 and not last:
                            if u == 1:
                                pe.wait_ge(q_lo, CHUNKS * t + 4)
                                x_job(nx, 0)
                            if u == 3:
                                pe.wait_ge(vt_cp, 2 * t + 1)
                                x_job(nx, 1)
                        if s == 0 and u >= 4 and not first:
                            if u == 4 and last:
                                pe.wait_ge(q_lo, CHUNKS * t + 4)
                            if u == 4 and not last:
                                pe.wait_ge(x_lo, TILES * nx + 1)
                            f_part(t - 1, 1, 0, part)
                        if s == 1 and u < 4 and not first:
                            if u == 0 and last:
                                pe.wait_ge(vt_cp, 2 * t + 1)
                            if u == 0 and not last:
                                pe.wait_ge(x_lo, TILES * nx + 2)
                            f_part(t - 1, 1, 1, part)
                        if s == 1 and u in (4, 6) and not last:
                            if first:
                                pe.wait_ge(x_lo, TILES * nx + u // 2 - 1)
                            else:
                                pe.wait_ge(f_add, TILES * t + u // 2 - 3)
                            x_job(nx, u // 2)
                        if s == 2 and u == 1:
                            if last:
                                pe.wait_ge(f_add, TILES * t - 1)
                            else:
                                pe.wait_ge(x_lo, TILES * nx + 3)
                            vt_job(t, 1)
                        if s == 2 and u >= 4 and not last:
                            q_part(nx, 0, part)
                        if s == 3 and not last:
                            if u == 0:
                                pe.wait_ge(vt_cp, 2 * t + 2)
                            if u == 1:
                                pe.wait_ge(q_lo, CHUNKS * nx + 1)
                            kv_part(nx, u % 2, u // 2)
                        if s == 4 and u >= 4:
                            if u == 4 and last:
                                pe.wait_ge(vt_cp, 2 * t + 2)
                            if u == 4 and not last:
                                pe.wait_ge(k_lo, nx + 1)
                            f_part(t, 0, 0, part)
                        if s == 5 and u < 4:
                            if u == 0 and last:
                                pe.wait_ge(f_add, TILES * t)
                            if u == 0 and not last:
                                pe.wait_ge(v_cp, nx + 1)
                            f_part(t, 0, 1, part)
                        if s == 5 and u >= 4 and not last:
                            if u == 4:
                                pe.wait_ge(f_add, TILES * t + 1)
                            q_part(nx, 1, part)
                        if s == 6 and u < 4 and not last:
                            if u == 0:
                                pe.wait_ge(f_add, TILES * t + 2)
                            q_part(nx, 2, part)
                        if s == 7 and u < 4 and not last:
                            if u == 0:
                                pe.wait_ge(q_lo, CHUNKS * nx + 2)
                            q_part(nx, 3, part)
                        if s == 7 and u == 5 and not last:
                            pe.wait_ge(q_lo, CHUNKS * nx + 3)
                            vt_job(nx, 0)

            blocks(pe, body)
            N = STEPS * BLOCKS
            pv_unit(N - 1, 3, 1, CHUNKS - 1)
            for qt in range(2):
                pe.wait_ge(f_add, TILES * BLOCKS - 2 - 1 + qt)
                for c in range(DC):
                    f_part(BLOCKS - 1, 1, qt, c)

            G, U, Y = bank[0:4:2], bank[1:4:2], bank[4:8]

            def x2_job(i):
                pe.wait_ge(xn2_ok, i + 1)
                if i < TILES:
                    if i == 0:
                        pe.wait_ge(f_add, TILES * BLOCKS)
                        pe.wait_ge(ob_ok, N)
                        pe.wait_ge(a_lo, N)
                elif i < 2 * TILES:
                    pe.wait_ge(x2_lo, i - TILES + 1)
                else:
                    pe.wait_ge(acc_ok, i - 2 * TILES + 1)
                for c in range(DC):
                    last = tr(Y[i % 4][:, c * P:(c + 1) * P], xn[:, i % 4, c * P:(c + 1) * P])
                last.then_inc(x2_tr, 1)

            def gate_up(k, b, par, ic, free):
                if free:
                    pe.wait_ge(hid_ok, IC * (k - 1) + ic + 1)
                tok = slice(b * BLOCK, (b + 1) * BLOCK)
                for o, bk in ((0, G[ic]), (GUW, U[ic])):
                    for c in range(DC):
                        w = slice(o + c * SC + ic * P, o + c * SC + (ic + 1) * P)
                        last = three(bk[:, :], w_h[par][:, w], w_l[par][:, w], x2T_h[:, c, tok], x2T_l[:, c, tok],
                                     c == 0, c == DC - 1)
                last.then_inc(gu_full, 1)

            def down(k, b, par, head):
                pe.wait_ge(h_lo, IC * (k + 1))
                for j in range(TILES):
                    if head and b < 3:
                        pe.wait_ge(x2_lo, TILES * (b + 1) + j + 1)
                    else:
                        pe.wait_ge(acc_ok, TILES * (k - 1) + j + 1)
                    tok = slice(j * P, (j + 1) * P)
                    for ic in range(IC):
                        w = slice(2 * GUW + ic * D, 2 * GUW + (ic + 1) * D)
                        last = three(Y[j][:, :], hT_h[:, b % 2, ic, tok], hT_l[:, b % 2, ic, tok],
                                     w_h[par][:, w], w_l[par][:, w], ic == 0, ic == IC - 1)
                    last.then_inc(y_full, 1)

            def router():
                pe.wait_ge(hid_ok, IC * BLOCKS * (SECTIONS - 2) - 1)
                pe.wait_ge(wr_ok, 2)
                for c in range(DC):
                    for part in (x2T_l, x2T_h):
                        for b in range(BLOCKS):
                            last = mm(bank[0][32 * b:32 * b + 32, :], wr[:, c, :],
                                      part[:, c, b * BLOCK:(b + 1) * BLOCK].bitcast(f32),
                                      start=c == 0 and part is x2T_l, stop=c == DC - 1 and part is x2T_h)
                last.then_inc(lg_mm, 1)
                pe.wait_ge(lg_cp, 1)
                for j in range(TILES):
                    last = tr(bank[1][:, j * P:(j + 1) * P], logT[:, j * P:(j + 1) * P])
                last.then_inc(lg_tr, 1)
                pe.wait_ge(top_ok, T // P)

            def section(sc, par):
                head = isinstance(sc, int) and sc == 0
                if isinstance(sc, int) and sc == SECTIONS - 2:
                    router()
                pe.wait_ge(w_split, sc + 1)
                for b in range(BLOCKS):
                    k = BLOCKS * sc + b
                    if head:
                        for j in range(TILES):
                            x2_job(TILES * b + j)
                        pe.wait_ge(x2_lo, TILES * (b + 1))
                    for ic in range(IC):
                        gate_up(k, b, par, ic, not (head and b == 0))
                    if not (head and b == 0):
                        down(k - 1, (b - 1) % BLOCKS, par if b else 1 - par, head)

            sections(pe, section)
            down(BLOCKS * SECTIONS - 1, BLOCKS - 1, 0, False)


_OUT = (B, S, D)


def kernel(**inputs):
    import concourse.bacc as bacc
    from concourse.bass_utils import run_bass_kernel_spmd

    def arr(name):
        return np.asarray(inputs[name])

    def rows(w):
        return np.ascontiguousarray(w.T.reshape(w.shape[1] // P, P, w.shape[0]).transpose(1, 0, 2)).reshape(P, -1)

    gate = np.concatenate([arr("L0_ffn_sh_gate"), arr("L0_ffn_r_gate")], 0)
    up = np.concatenate([arr("L0_ffn_sh_up"), arr("L0_ffn_r_up")], 0)
    down = np.concatenate([arr("L0_ffn_sh_down"), arr("L0_ffn_r_down")], 1)
    w_ffn = np.stack([
        np.concatenate([rows(gate[i * SC:(i + 1) * SC]), rows(up[i * SC:(i + 1) * SC]),
                        rows(down[:, i * SC:(i + 1) * SC])], 1) for i in range(SECTIONS)])
    ctx_t = arr("ctx_2048").reshape(BLOCKS, BLOCK, DC, P).transpose(0, 2, 3, 1)
    wfc = arr("L0_xattn_Wfc").T.reshape(DC, 2, RH, DH, D).transpose(2, 1, 3, 0, 4)
    arrays = {
        "x": arr("x").reshape(T, D),
        "ctxT": ctx_t,
        "wq": rows(arr("L0_xattn_Wq")), "wk": rows(arr("L0_xattn_Wk")), "wv": rows(arr("L0_xattn_Wv")),
        "wfc": np.ascontiguousarray(wfc).reshape(P, -1), "bfc": arr("L0_xattn_bfc"),
        "g_x": arr("g_xattn"), "g_f": arr("g_ffn"),
        "w_ffn": w_ffn, "w_r": rows(arr("L0_ffn_router_weight")),
    }
    arrays = {k: np.ascontiguousarray(v) for k, v in arrays.items()}
    nc = bacc.Bacc("TRN2", target_bir_lowering=False, num_devices=1)
    args = {k: nc.dram_tensor(k, v.shape, mybir.dt.from_np(v.dtype), kind="ExternalInput").ap()
            for k, v in arrays.items()}
    out = nc.dram_tensor("out", (T, D), mybir.dt.float32, kind="ExternalOutput").ap()
    build(nc, out=out, **args)
    r = run_bass_kernel_spmd(nc, [arrays], core_ids=[0])
    return r.results[0]["out"].reshape(_OUT)
```

```python
import numpy as np
import concourse.bass as bass
from concourse import mybir
from contextlib import ExitStack

B, S, D = 8, 256, 512
HEADS, GROUPS, DH = 32, 8, 16
SHARED, ROUTED, EXPERTS = 2048, 256, 8
P = 128
T = B * S
DC = D // P
BLOCK = 2 * S
BLOCKS = T // BLOCK
TILES = BLOCK // P
HC = P // DH
CHUNKS = HEADS // HC
STEPS = 2 * CHUNKS
RH = HEADS // GROUPS
KV = GROUPS * DH
UNITS = 8
CONSTS = 2
SM = P // 2 + 1
MROW = SM
ST = MROW + 1
VW = 32
SC = 256
SECTIONS = (SHARED + ROUTED) // SC
IC = SC // P
GUW = DC * SC
SECW = 2 * GUW + IC * D
EPS = 1e-5


def build(nc, x, ctxT, wq, wk, wv, wfc, bfc, g_x, g_f, w_ffn, w_r, out):
    f32, f32r = mybir.dt.float32, mybir.dt.float32r
    ALU, ACT, AX = mybir.AluOpType, mybir.ActivationFunctionType, mybir.AxisListType
    q_scr = nc.dram_tensor("q_scr", (2, BLOCKS, CHUNKS, P, BLOCK), f32, kind="Internal").ap()
    k_scr = nc.dram_tensor("k_scr", (2, BLOCKS, P, BLOCK), f32, kind="Internal").ap()

    with ExitStack() as ctx:
        def sem(name):
            return ctx.enter_context(nc.semaphore(name))

        def sb(name, shape, dt=f32, where=ctx):
            return where.enter_context(nc.sbuf_tensor(name, shape, dt))

        xa = sb("xa", [P, T // P, D])
        ident = sb("ident", [P, P])
        tgx = sb("tgx", [P, 1])
        tgf = sb("tgf", [P, 1])
        gates = sb("gates", [P, 2])
        mv = sb("mv", [P, 2, T // P, 2])
        rstd = sb("rstd", [P, 2, T // P])
        nmr = sb("nmr", [P, 2, T // P])
        power = sb("power", [P, T // P])
        stats = sb("stats", [P, T // P, 6])
        xn = sb("xn", [P, 4, D])
        wr_raw = sb("wr_raw", [P, DC * EXPERTS])
        wr = sb("wr", [P, DC, 32])

        att = ExitStack()
        wq_h = sb("wq_h", [P, DC, D], f32r, att)
        wq_l = sb("wq_l", [P, DC, D], f32r, att)
        wkv_h = sb("wkv_h", [P, 2, DC, KV], f32r, att)
        wkv_l = sb("wkv_l", [P, 2, DC, KV], f32r, att)
        xnT_h = sb("xnT_h", [P, DC, BLOCK], f32r, att)
        xnT_l = sb("xnT_l", [P, DC, BLOCK], f32r, att)
        cx_h = sb("cx_h", [P, 2, BLOCK], f32r, att)
        cx_l = sb("cx_l", [P, 2, BLOCK], f32r, att)
        vT = sb("vT", [P, BLOCK], f32, att)
        qx_h = sb("qx_h", [P, 2, BLOCK], f32r, att)
        kx_h = sb("kx_h", [P, BLOCK], f32r, att)
        kx_l = sb("kx_l", [P, BLOCK], f32r, att)
        qx_l = sb("qx_l", [P, 2, BLOCK], f32r, att)
        cx_raw = sb("cx_raw", [P, 2, BLOCK], f32, att)
        q_st = sb("q_st", [P, CHUNKS, HC, S], f32r, att)
        k_st = sb("k_st", [P, 2, GROUPS, S], f32r, att)
        wfc_h = sb("wfc_h", [P, DC, D], f32r, att)
        wfc_l = sb("wfc_l", [P, DC, D], f32r, att)
        early = ExitStack()
        wfc_raw = sb("wfc_raw", [P, DC * D], f32, early)
        early.close()
        aT_h = sb("aT_h", [P, DC, S], f32r, att)
        aT_l = sb("aT_l", [P, DC, S], f32r, att)
        probs = sb("probs", [P, 4, RH, S], f32, att)
        vals = sb("vals", [P, 2, S // P, GROUPS, VW], f32, att)
        oB = sb("oB", [P, 2 * S // VW, VW], f32, att)
        oN = sb("oN", [P, S // VW, 2 * DH], f32, att)
        aT = sb("aT", [P, S], f32, att)
        tbias = sb("tbias", [P, D], f32, att)
        mcol = sb("mcol", [P, 2, 16], f32, att)
        mT = sb("mT", [16, P], f32r, att)
        rden = sb("rden", [P, 16], f32, att)
        att.close()

        def a_split(high, last_batch):
            if last_batch:
                part = qx_h if high else qx_l
                return part[:, :, :].rearrange("p a (b q) -> p (a b) q", q=S)
            return aT_h if high else aT_l

        pflat = probs[:, :, :, :].rearrange("p a r s -> p (a r s)")
        wq_raw, wkv_raw = pflat[:, 0:DC * D], pflat[:, DC * D:DC * D + 2 * DC * KV]

        w_raw = sb("w_raw", [P, 2, SECW])
        w_h0 = sb("w_h0", [P, SECW], f32r)
        w_l0 = sb("w_l0", [P, SECW], f32r)
        x2T_h = sb("x2T_h", [P, DC, T], f32r)
        x2T_l = sb("x2T_l", [P, DC, T], f32r)
        w_h1 = sb("w_h1", [P, SECW], f32r)
        w_l1 = sb("w_l1", [P, SECW], f32r)
        w_h, w_l = (w_h0, w_h1), (w_l0, w_l1)
        hT_h = sb("hT_h", [P, 2, IC, BLOCK], f32r)
        hT_l = sb("hT_l", [P, 2, IC, BLOCK], f32r)
        silu = sb("silu", [P, IC, BLOCK])
        hid = sb("hid", [P, IC, BLOCK])
        logT = sb("logT", [P, BLOCK])
        top = sb("top", [P, T // P, EXPERTS])
        comb = sb("comb", [P, 4, T // P])

        bank = [ctx.enter_context(nc.psum_tensor(f"bank{i}", [P, 512], f32)) for i in range(8)]
        STB, OTB, TPB, PJ = bank[2:4], bank[4], bank[5], bank[6:8]

        in_x = [sem(f"in_x{i}") for i in range(BLOCKS)]
        in_wkv, in_wq, in_wfc, in_vectors = sem("in_wkv"), sem("in_wq"), sem("in_wfc"), sem("in_vectors")
        in_cx = [sem("in_cx0"), sem("in_cx1")]
        in_w = [sem("in_w0"), sem("in_w1")]
        q_wr = [sem(f"q_wr{c}") for c in range(CHUNKS)]
        k_wr = sem("k_wr")
        q_rd = [sem(f"q_rd{c}") for c in range(CHUNKS)]
        k_rd = [sem("k_rd0"), sem("k_rd1")]
        m_rd = sem("m_rd")
        stored = sem("stored")
        consts, ident_ok, wq_ok, wkv_ok, wfc_ok = sem("consts"), sem("ident_ok"), sem("wq_ok"), sem("wkv_ok"), sem("wfc_ok")
        w_hi = sem("w_hi")
        gate_ok, tb_ok, pool_waits = sem("gate_ok"), sem("tb_ok"), sem("pool_waits")
        ln1_stats, ln1_var, var_ok, rs_ok, nm_ok = sem("ln1_stats"), sem("ln1_var"), sem("var_ok"), sem("rs_ok"), sem("nm_ok")
        cx_hi, cx_split, cx_used = sem("cx_hi"), sem("cx_split"), sem("cx_used")
        xn_ok, x_tr, x_hi, x_lo, xb_ok = sem("xn_ok"), sem("x_tr"), sem("x_hi"), sem("x_lo"), sem("xb_ok")
        q_pr, q_hi, q_lo = sem("q_pr"), sem("q_hi"), sem("q_lo")
        k_pr, k_hi, k_lo = sem("k_pr"), sem("k_hi"), sem("k_lo")
        v_cp, vt_tr, vt_cp = sem("v_cp"), sem("vt_tr"), sem("vt_cp")
        f_mm, f_add, ln2_stats, ln2_var = sem("f_mm"), sem("f_add"), sem("ln2_stats"), sem("ln2_var")
        sm_full, max_ok = sem("sm_full"), sem("max_ok")
        mt_tr, mt_cp = sem("mt_tr"), sem("mt_cp")
        st_full, exp_ok, pv_ok = sem("st_full"), sem("exp_ok"), sem("pv_ok")
        ob_ok, rden_ok, norm_ok, at_ok, a_hi, a_lo = (sem("ob_ok"), sem("rden_ok"), sem("norm_ok"), sem("at_ok"),
                                                      sem("a_hi"), sem("a_lo"))
        ffn_w_hi, ffn_w_ok, rs2_ok, nm2_ok = sem("ffn_w_hi"), sem("ffn_w_ok"), sem("rs2_ok"), sem("nm2_ok")
        xn2_ok, x2_tr, x2_hi, x2_lo = sem("xn2_ok"), sem("x2_tr"), sem("x2_hi"), sem("x2_lo")
        gu_full, silu_ok, hid_ok, h_hi, h_lo = sem("gu_full"), sem("silu_ok"), sem("hid_ok"), sem("h_hi"), sem("h_lo")
        y_full, acc_ok = sem("y_full"), sem("acc_ok")
        wr_ok, lg_mm, lg_cp, lg_tr, top_ok, comb_ok, e_ok, order = (sem("wr_ok"), sem("lg_mm"), sem("lg_cp"), sem("lg_tr"),
                                                                    sem("top_ok"), sem("comb_ok"), sem("e_ok"), sem("order"))

        LOTS = (0, TILES, (BLOCKS - 1) * TILES, BLOCKS * TILES)

        def sm_banks(n):
            return 4 if isinstance(n, int) and n < 2 else 2

        def x_bank(tb, j):
            return bank[j] if isinstance(tb, int) and tb == 0 else PJ[j % 2]

        def split_unit(s):
            return 5 if s in (3, 6, 7) else 4

        def x2_bank(i):
            return bank[i] if i < TILES else bank[4 + i % 4]

        block = ctx.enter_context(nc.Block())

        def blocks(eng, body):
            body(0, True, False)
            with eng.Fori(1, BLOCKS - 1) as t:
                body(t, False, False)
            body(BLOCKS - 1, False, True)

        def sections(eng, body):
            body(0, 0)
            with eng.Fori(0, (SECTIONS - 3) // 2) as i:
                body(2 * i + 1, 1)
                body(2 * i + 2, 0)
            body(SECTIONS - 2, 1)
            body(SECTIONS - 1, 0)

        @block.sync
        def _(sp):
            def r(ap):
                return ap.bitcast(f32)

            def load_cx(tb, c):
                if not (isinstance(tb, int) and tb == 0 and c < 2):
                    sp.wait_ge(cx_split, DC * tb + c - 1)
                sp.dma_start(cx_raw[:, c % 2, :], ctxT[tb, c, :, :]).then_inc(in_cx[c % 2], 16)

            def write_q_high(tb, oc):
                sp.wait_ge(q_hi, CHUNKS * tb + oc + 1)
                sp.dma_start(q_scr[0, tb, oc, :, :], r(qx_h[:, oc % 2, :])).then_inc(q_wr[oc], 16)

            def write_q_low(tb, oc):
                sp.wait_ge(q_lo, CHUNKS * tb + oc + 1)
                sp.dma_start(q_scr[1, tb, oc, :, :], r(qx_l[:, oc % 2, :])).then_inc(q_wr[oc], 16)

            def read_q(tb, bb, c, n, fresh):
                if not fresh:
                    sp.wait_ge(st_full, UNITS * n)
                sp.wait_ge(q_wr[c], 32 * (tb + 1))
                for row, part in ((0, 0), (DH, 0), (2 * DH, 1)):
                    src = q_scr[part, tb, c, :, bb * S:(bb + 1) * S].rearrange("(h d) q -> d h q", d=DH)
                    sp.dma_start(r(q_st[row:row + DH, c, :, :]), src).then_inc(q_rd[c], 16)

            def write_k(tb):
                sp.wait_ge(k_hi, tb + 1)
                sp.wait_ge(k_lo, tb + 1)
                sp.dma_start(k_scr[0, tb, :, :], r(kx_h[:, :])).then_inc(k_wr, 16)
                sp.dma_start(k_scr[1, tb, :, :], r(kx_l[:, :])).then_inc(k_wr, 16)

            def read_k(tb, bb):
                sp.wait_ge(k_wr, 32 * (tb + 1))
                for row, part in ((0, 0), (DH, 1), (2 * DH, 0)):
                    src = k_scr[part, tb, :, bb * S:(bb + 1) * S].rearrange("(g d) s -> d g s", d=DH)
                    sp.dma_start(r(k_st[row:row + DH, bb, :, :]), src).then_inc(k_rd[bb], 16)

            def put_max(n, slot):
                sp.wait_ge(mt_cp, n + 1)
                for qt in range(2):
                    sp.dma_start(r(q_st[MROW:MROW + 1, slot, :, qt * P:(qt + 1) * P]),
                                 r(mT[qt * HC:(qt + 1) * HC, :])).then_inc(m_rd, 16)

            x_v = x.rearrange("(t j p) d -> t p j d", p=P, j=TILES)
            sp.dma_start(xa[:, 0:TILES, :], x_v[0]).then_inc(in_x[0], 16)
            sp.dma_start(wkv_raw[:, 0:DC * KV], wk).then_inc(in_wkv, 16)
            sp.dma_start(wkv_raw[:, DC * KV:2 * DC * KV], wv).then_inc(in_wkv, 16)
            load_cx(0, 0)
            load_cx(0, 1)
            sp.dma_start(wq_raw, wq).then_inc(in_wq, 16)
            load_cx(0, 2)
            load_cx(0, 3)
            sp.dma_start(tbias[:, :], bfc.partition_broadcast(P)).then_inc(in_vectors, 16)
            sp.dma_start(gates[:, 0:1], g_x.partition_broadcast(P)).then_inc(in_vectors, 16)
            sp.dma_start(gates[:, 1:2], g_f.partition_broadcast(P)).then_inc(in_vectors, 16)
            sp.dma_start(wr_raw[:, :], w_r).then_inc(in_vectors, 16)
            for t in (1, 2):
                sp.dma_start(xa[:, TILES * t:TILES * (t + 1), :], x_v[t]).then_inc(in_x[t], 16)
            sp.wait_ge(consts, CONSTS)
            write_k(0)
            write_q_high(0, 0)
            write_q_low(0, 0)
            read_k(0, 0)
            write_q_high(0, 1)
            write_q_low(0, 1)
            read_q(0, 0, 0, 0, True)
            read_q(0, 0, 1, 0, True)
            write_q_high(0, 2)
            write_q_low(0, 2)
            read_q(0, 0, 2, 0, True)
            sp.dma_start(wfc_raw[:, :], wfc).then_inc(in_wfc, 16)
            put_max(0, 0)
            write_q_high(0, 3)
            write_q_low(0, 3)

            def body(t, first, last):
                for s in range(STEPS):
                    n = STEPS * t + s
                    if s + 3 < STEPS or not last and s != 6:
                        e = s + 3
                        tb = t if e < STEPS else t + 1
                        read_q(tb, e % STEPS // CHUNKS, e % CHUNKS, n, first and s == 0)
                    if not last:
                        if s == 4:
                            write_k(t + 1)
                        if s == 6:
                            write_q_low(t + 1, 1)
                    if not last or s + 1 < STEPS:
                        put_max(n + 1, (s + 1) % CHUNKS)
                    if s == 0:
                        if not first:
                            sp.wait_ge(st_full, UNITS * n)
                        read_k(t, 1)
                    if s in (0, 2) and not last:
                        load_cx(t + 1, s)
                        load_cx(t + 1, s + 1)
                    if s == 0 and first:
                        sp.dma_start(xa[:, T // P - TILES:T // P, :], x_v[BLOCKS - 1]).then_inc(in_x[BLOCKS - 1], 16)
                    if not last:
                        if s == 3:
                            write_q_high(t + 1, 0)
                            write_q_low(t + 1, 0)
                        if s == 5:
                            write_q_high(t + 1, 1)
                        if s == 4:
                            read_k(t + 1, 0)
                        if s == 6:
                            read_q(t + 1, 0, 1, n, False)
                            write_q_high(t + 1, 2)
                            write_q_low(t + 1, 2)
                        if s == 7:
                            write_q_high(t + 1, 3)
                            write_q_low(t + 1, 3)
                    elif s == 0:
                        sp.wait_ge(q_lo, CHUNKS * BLOCKS)
                        sp.wait_ge(k_lo, BLOCKS)
                        sp.wait_ge(v_cp, BLOCKS)
                        for sc in range(2):
                            sp.dma_start(w_raw[:, sc, :], w_ffn[sc, :, :]).then_inc(in_w[sc], 16)

            blocks(sp, body)

            def section(sc, par):
                if isinstance(sc, int) and sc + 2 >= SECTIONS:
                    return
                sp.wait_ge(ffn_w_ok, sc + 1)
                sp.dma_start(w_raw[:, par, :], w_ffn[sc + 2, :, :]).then_inc(in_w[par], 16)

            body_n = SECTIONS - 2
            section(0, 0)
            with sp.Fori(0, (body_n - 1) // 2) as i:
                section(2 * i + 1, 1)
                section(2 * i + 2, 0)
            o_v = out.rearrange("(i p) d -> i p d", p=P)
            for i in range(T // P):
                sp.wait_ge(acc_ok, TILES * BLOCKS * (SECTIONS - 1) + i + 1)
                sp.dma_start(o_v[i], xa[:, i, :]).then_inc(stored, 16)
            sp.wait_ge(stored, 16 * (T // P))

        @block.gpsimd
        def _(pool):
            g = nc.gpsimd

            def cx_low(tb, c):
                pool.wait_ge(cx_hi, DC * tb + c + 1)
                g.tensor_tensor(cx_l[:, c % 2, :], cx_raw[:, c % 2, :], cx_h[:, c % 2, :].bitcast(f32),
                                ALU.subtract).then_inc(cx_split, 1)

            def root(lot, a, b):
                g.tensor_scalar(rstd[:, lot, a:b], mv[:, lot, a:b, 1], EPS, 0.0, ALU.add, ALU.add).then_inc(var_ok, 1)

            g.memset(ident[:, :], 0.0).then_inc(order, 1)
            pool.wait_ge(order, 1)
            g.affine_select(out=ident[:, :], in_=ident[:, :], compare_op=ALU.not_equal, fill=1.0, base=0,
                            pattern=[[-1, P]], channel_multiplier=1).then_inc(ident_ok, 1)
            g.memset(power[:, :], -0.5)
            g.memset(vals[:, :, :, :, DH:VW], 1.0).then_inc(order, 1)
            pool.wait_ge(order, 2)
            g.memset(q_st[0:SM, :, :, :].bitcast(f32), 0.0).then_inc(consts, 1)
            def deviations(lot):
                a, b = LOTS[lot], LOTS[lot + 1]
                pool.wait_ge(ln1_var, b)
                root(0, a, b)
                pool.wait_ge(var_ok, lot + 1)
                g.tensor_tensor(rstd[:, 0, a:b], rstd[:, 0, a:b], power[:, 0:b - a], ALU.pow).then_inc(rs_ok, 1)

            deviations(0)
            deviations(1)

            def add_bias(tb):
                pool.wait_ge(tb_ok, 1)
                for j in range(TILES):
                    pool.wait_ge(xn_ok, TILES * tb + j + 1)
                    tile = xa[:, bass.ds(TILES * tb + j, 1), :].rearrange("p a d -> p (a d)")
                    g.tensor_tensor(tile, tile, tbias[:, :], ALU.add).then_inc(xb_ok, 1)

            add_bias(0)

            def body(t, first, last):
                for s in range(STEPS):
                    n = STEPS * t + s
                    if last:
                        continue
                    if s in (1, 3):
                        cx_low(t + 1, s - 1)
                        cx_low(t + 1, s)
                    if first and s == 4:
                        deviations(2)
                    if s == 4:
                        add_bias(t + 1)

            def split_w(sc, par):
                pool.wait_ge(in_w[par], 8 * (sc - par) + 16)
                if isinstance(sc, int) and sc == 0:
                    pool.wait_ge(q_lo, CHUNKS * BLOCKS)
                    pool.wait_ge(v_cp, BLOCKS)
                if isinstance(sc, int) and sc == 1:
                    pool.wait_ge(f_add, TILES * BLOCKS)
                    pool.wait_ge(a_lo, STEPS * BLOCKS)
                if not isinstance(sc, int) or sc >= 2:
                    pool.wait_ge(y_full, TILES * BLOCKS * (sc - 1))
                pool.sem_inc(pool_waits)
                g.tensor_copy(w_h[par][:, :], w_raw[:, par, :]).then_inc(ffn_w_hi, 1)
                pool.wait_ge(ffn_w_hi, sc + 1)
                g.tensor_tensor(w_l[par][:, :], w_raw[:, par, :], w_h[par][:, :].bitcast(f32),
                                ALU.subtract).then_inc(ffn_w_ok, 1)

            blocks(pool, body)
            split_w(0, 0)
            for lot, (a, b) in enumerate(((0, 12), (12, 16))):
                pool.wait_ge(ln2_var, b)
                root(1, a, b)
                pool.wait_ge(var_ok, lot + len(LOTS))
                g.tensor_tensor(rstd[:, 1, a:b], rstd[:, 1, a:b], power[:, 0:b - a], ALU.pow).then_inc(rs2_ok, 1)
            split_w(1, 1)
            with pool.Fori(0, (SECTIONS - 3) // 2) as i:
                split_w(2 * i + 2, 0)
                split_w(2 * i + 3, 1)
            split_w(SECTIONS - 1, 0)

        @block.scalar
        def _(act):
            def copy(out, in_):
                return nc.scalar.activation(out, in_, ACT.Copy)

            def normalise(lot, i, slot):
                tile = xa[:, bass.ds(i, 1), :].rearrange("p a d -> p (a d)")
                return nc.scalar.activation(xn[:, slot, :], tile, ACT.Identity,
                                            bias=nmr[:, lot, bass.ds(i, 1)], scale=rstd[:, lot, bass.ds(i, 1)])

            def xn_tile(tb, j):
                if not (isinstance(tb, int) and tb == 0):
                    act.wait_ge(x_tr, TILES * (tb - 1) + j + 1)
                if j == 0:
                    act.wait_ge(nm_ok, tb + 1 if isinstance(tb, int) and tb < 2 else len(LOTS) - 1)
                normalise(0, TILES * tb + j, j).then_inc(xn_ok, 1)

            def cx_high(tb, c):
                act.wait_ge(in_cx[c % 2], 16 * (2 * tb + c // 2 + 1))
                if not (isinstance(tb, int) and tb == 0 and c < 2):
                    act.wait_ge(cx_used, DC * tb + c - 1)
                copy(cx_h[:, c % 2, :], cx_raw[:, c % 2, :]).then_inc(cx_hi, 1)

            def x_high(tb, j):
                act.wait_ge(x_tr, TILES * tb + j + 1)
                if not (isinstance(tb, int) and tb == 0):
                    act.wait_ge(q_pr, CHUNKS * tb)
                copy(xnT_h[:, :, j * P:(j + 1) * P],
                     x_bank(tb, j)[:, :].rearrange("p (c q) -> p c q", c=DC)).then_inc(x_hi, 1)

            def q_high(tb, oc):
                act.wait_ge(q_pr, CHUNKS * tb + oc + 1)
                if isinstance(tb, int) and tb == 0:
                    if oc >= 2:
                        act.wait_ge(q_wr[oc - 2], 32)
                else:
                    act.wait_ge(q_wr[(oc + 2) % 4], 32 * (tb + 1) if oc >= 2 else 32 * tb)
                copy(qx_h[:, oc % 2, :], PJ[(oc + 1) % 2][:, :]).then_inc(q_hi, 1)

            def k_high(tb):
                act.wait_ge(k_pr, tb + 1)
                if not (isinstance(tb, int) and tb == 0):
                    act.wait_ge(k_wr, 32 * tb)
                copy(kx_h[:, :], PJ[0][:, :]).then_inc(k_hi, 1)

            def v_copy(tb):
                act.wait_ge(cx_used, DC * (tb + 1))
                if not (isinstance(tb, int) and tb == 0):
                    act.wait_ge(vt_tr, 2 * tb)
                copy(vT[:, :], PJ[1][:, :]).then_inc(v_cp, 1)

            def vt_copy(tb, bb):
                act.wait_ge(vt_tr, 2 * tb + bb + 1)
                if not (isinstance(tb, int) and tb == 0):
                    act.wait_ge(pv_ok, 4 * (STEPS * (tb - 1) + CHUNKS * (bb + 1)))
                copy(vals[:, bb, :, :, 0:DH],
                     PJ[(bb + 1) % 2][:, 0:S].rearrange("p (k g d) -> p k g d", k=S // P, g=GROUPS)).then_inc(vt_cp, 1)

            def m_copy(n):
                act.wait_ge(mt_tr, n + 1)
                if not (isinstance(n, int) and n == 0):
                    act.wait_ge(m_rd, 32 * n)
                nc.scalar.activation(mT[:, :], TPB[0:16, 0:P], ACT.Copy, scale=-1.0).then_inc(mt_cp, 1)

            def wq_high(half):
                act.wait_ge(in_wq, 16)
                w = slice(half * DC * D // 2, (half + 1) * DC * D // 2)
                copy(wq_h[:, :, :].rearrange("p c n -> p (c n)")[:, w], wq_raw[:, w]).then_inc(w_hi, 1)

            act.wait_ge(in_wkv, 32)
            copy(wkv_h[:, :, :, :].rearrange("p a c n -> p (a c n)"), wkv_raw).then_inc(w_hi, 1)
            cx_high(0, 0)
            cx_high(0, 1)
            xn_tile(0, 0)
            xn_tile(0, 1)
            wq_high(0)
            cx_high(0, 2)
            xn_tile(0, 2)
            cx_high(0, 3)
            xn_tile(0, 3)
            x_high(0, 0)
            x_high(0, 1)
            wq_high(1)
            x_high(0, 2)
            x_high(0, 3)
            k_high(0)
            v_copy(0)
            act.wait_ge(in_vectors, 64)
            nc.scalar.activation(tgx[:, :], gates[:, 0:1], ACT.Tanh).then_inc(gate_ok, 1)
            nc.scalar.activation(tgf[:, :], gates[:, 1:2], ACT.Tanh).then_inc(gate_ok, 1)
            q_high(0, 0)
            q_high(0, 1)
            q_high(0, 2)
            m_copy(0)
            vt_copy(0, 0)
            act.wait_ge(in_wfc, 16)
            copy(wfc_h[:, :, :].rearrange("p c n -> p (c n)"), wfc_raw[:, :]).then_inc(w_hi, 1)
            q_high(0, 3)
            act.wait_ge(wq_ok, 2)
            act.wait_ge(wkv_ok, 1)

            def a_high(n, c, batch):
                act.wait_ge(at_ok, n + 1)
                last_batch = isinstance(batch, int) and batch == B - 1
                if isinstance(n, int) and n == 0:
                    act.wait_ge(wfc_ok, 1)
                if last_batch:
                    for oc in (2, 3):
                        act.wait_ge(q_wr[oc], 32 * BLOCKS)
                elif not (isinstance(batch, int) and batch == 0):
                    act.wait_ge(f_mm, 2 * batch)
                copy(a_split(True, last_batch)[:, c, :], aT[:, :]).then_inc(a_hi, 1)

            def x2_tile(i):
                if i == 0 or i == 12:
                    act.wait_ge(nm2_ok, 1 if i == 0 else 2)
                if i < TILES:
                    act.wait_ge(x_tr, T // P - TILES + i + 1)
                else:
                    act.wait_ge(x2_tr, i - TILES + 1)
                normalise(1, i, i % 4).then_inc(xn2_ok, 1)

            def body(t, first, last):
                nx = t + 1
                for s in range(STEPS):
                    n = STEPS * t + s
                    for u in range(UNITS):
                        p = u // 2
                        act.wait_ge(st_full, UNITS * n + u + 1)
                        if u % 2 == 0 and not (first and s == 0):
                            act.wait_ge(pv_ok, 4 * (n - 1) + p + 1)
                        nc.scalar.activation(probs[:, p, 2 * (u % 2):2 * (u % 2) + 2, :],
                                             STB[u % 2][:, :].rearrange("p (r q) -> p r q", r=2),
                                             ACT.Exp, scale=float(DH) ** -0.5).then_inc(exp_ok, 1)
                        if s == 0 and u == 2 and not last:
                            x_high(nx, 0)
                        if u == 2 and (not last or s + 1 < STEPS):
                            m_copy(n + 1)
                        if u == split_unit(s) and not (first and s == 0):
                            a_high(n - 1, (s - 1) % CHUNKS, 2 * t + (s - 1) // CHUNKS)
                        if s == 2 and u == 2:
                            vt_copy(t, 1)
                        if last and (s, u) in ((6, 3), (6, 7), (7, 3), (7, 7)):
                            x2_tile(2 * (s - 6) + u // 7)
                        if last:
                            continue
                        if s == 0 and u < 2:
                            xn_tile(nx, u)
                        if s == 0 and u == 5:
                            x_high(nx, 1)
                        if s == 1 and u in (1, 3):
                            xn_tile(nx, 2 + u // 2)
                        if s == 1 and u in (2, 6):
                            cx_high(nx, u // 4)
                        if s == 1 and u in (5, 7):
                            x_high(nx, u // 2)
                        if s == 2 and u == 7:
                            q_high(nx, 0)
                        if s == 3 and u in (2, 4):
                            cx_high(nx, 1 + u // 2)
                        if s == 3 and u == 7:
                            k_high(nx)
                        if s == 4 and u == 6:
                            v_copy(nx)
                        if s == 5 and u == 7:
                            q_high(nx, 1)
                        if s == 6 and u == 4:
                            q_high(nx, 2)
                        if s == 7 and u == 4:
                            q_high(nx, 3)
                        if s == 7 and u == 6:
                            vt_copy(nx, 0)

            blocks(act, body)

            def x2_high(i):
                act.wait_ge(x2_tr, i + 1)
                copy(x2T_h[:, :, i * P:(i + 1) * P],
                     x2_bank(i)[:, :].rearrange("p (c q) -> p c q", c=DC)).then_inc(x2_hi, 1)

            x2_high(0)
            x2_high(1)
            a_high(STEPS * BLOCKS - 1, CHUNKS - 1, B - 1)
            x2_high(2)
            x2_high(3)

            def section(sc, par):
                head = isinstance(sc, int) and sc == 0
                if isinstance(sc, int) and sc == SECTIONS - 1:
                    act.wait_ge(top_ok, T // P)
                    act.wait_ge(comb_ok, 1)
                    nc.scalar.activation(comb[:, 1, :], comb[:, 0, :], ACT.Exp).then_inc(e_ok, 1)
                for b in range(BLOCKS):
                    k = BLOCKS * sc + b
                    ahead = range(TILES * (b + 1), TILES * (b + 2)) if head and b + 1 < BLOCKS else ()
                    for i in ahead:
                        x2_tile(i)
                    for ic in range(IC):
                        act.wait_ge(gu_full, IC * k + ic + 1)
                        if not (head and b == 0):
                            act.wait_ge(hid_ok, IC * (k - 1) + ic + 1)
                        nc.scalar.activation(silu[:, ic, :], bank[2 * ic][:, :], ACT.Silu).then_inc(silu_ok, 1)
                        if ic == 0:
                            for i in ahead:
                                x2_high(i)
                    for ic in range(IC):
                        act.wait_ge(hid_ok, IC * k + ic + 1)
                        if not (head and b < 2):
                            act.wait_ge(y_full, TILES * (k - 1))
                        copy(hT_h[:, b % 2, ic, :], hid[:, ic, :]).then_inc(h_hi, 1)

            sections(act, section)

        @block.vector
        def _(dve):
            v = nc.vector

            def low(out, psum, high):
                return v.tensor_tensor(out, psum, high.bitcast(f32), ALU.subtract)

            def aggregate(lot, i, done):
                v.bn_aggr(mv[:, lot, i, :], stats[:, i, :]).then_inc(done, 1)

            def x_low(tb, j):
                dve.wait_ge(x_hi, TILES * tb + j + 1)
                sl = slice(j * P, (j + 1) * P)
                low(xnT_l[:, :, sl], x_bank(tb, j)[:, :].rearrange("p (c q) -> p c q", c=DC),
                    xnT_h[:, :, sl]).then_inc(x_lo, 1)

            def q_low(tb, oc):
                dve.wait_ge(q_hi, CHUNKS * tb + oc + 1)
                low(qx_l[:, oc % 2, :], PJ[(oc + 1) % 2][:, :], qx_h[:, oc % 2, :]).then_inc(q_lo, 1)

            def k_low(tb):
                dve.wait_ge(k_hi, tb + 1)
                low(kx_l[:, :], PJ[0][:, :], kx_h[:, :]).then_inc(k_lo, 1)

            def maximum(n, u, par):
                qt, g2, half = u // 2 % 2, u // 4, u % 2
                dve.wait_ge(sm_full, UNITS * n + u + 1)
                if u == 0 and not (isinstance(n, int) and n < 2):
                    dve.wait_ge(mt_tr, n - 1)
                at = qt * HC + g2 * RH + half * 2
                v.tensor_reduce(mcol[:, par, at:at + 2], bank[u % sm_banks(n)][:, :].rearrange("p (r k) -> p r k", r=2),
                                AX.X, ALU.max).then_inc(max_ok, 1)

            def tile_of(f):
                return xa[:, bass.ds(f, 1), :].rearrange("p a d -> p (a d)")

            def f_sum(t, bb, qt):
                f = TILES * t + 2 * bb + qt
                dve.wait_ge(f_mm, f + 1)
                dve.wait_ge(xb_ok, f + 1)
                v.scalar_tensor_tensor(tile_of(f), PJ[qt][:, :], tgx[:, :], tile_of(f),
                                       ALU.mult, ALU.add).then_inc(f_add, 1)

            def f_stats(t, bb, qt):
                f = TILES * t + 2 * bb + qt
                dve.wait_ge(f_add, f + 1)
                dve.wait_ge(ln1_var, T // P)
                v.bn_stats(stats[:, bass.ds(f, 1), :].rearrange("p a k -> p (a k)"), tile_of(f)).then_inc(ln2_stats, 1)

            def norm_rows(lot):
                a, b = LOTS[lot], LOTS[lot + 1]
                dve.wait_ge(rs_ok, lot + 1)
                v.scalar_tensor_tensor(nmr[:, 0, a:b], mv[:, 0, a:b, 0], -1.0, rstd[:, 0, a:b],
                                       ALU.mult, ALU.mult).then_inc(nm_ok, 1)

            def statistics(t):
                dve.wait_ge(in_x[t], 16)
                for i in range(TILES * t, TILES * (t + 1)):
                    tile_stats(i)
                aggregates(t)

            def tile_stats(i):
                v.bn_stats(stats[:, i, :], xa[:, i, :]).then_inc(ln1_stats, 1)

            def aggregates(t):
                dve.wait_ge(ln1_stats, TILES * (t + 1))
                for i in range(TILES * t, TILES * (t + 1)):
                    aggregate(0, i, ln1_var)

            def cx_low(c):
                dve.wait_ge(cx_hi, c + 1)
                low(cx_l[:, c % 2, :], cx_raw[:, c % 2, :], cx_h[:, c % 2, :]).then_inc(cx_split, 1)

            def wq_low(half):
                dve.wait_ge(w_hi, half + 2)
                w = slice(half * DC * D // 2, (half + 1) * DC * D // 2)
                low(wq_l[:, :, :].rearrange("p c n -> p (c n)")[:, w], wq_raw[:, w],
                    wq_h[:, :, :].rearrange("p c n -> p (c n)")[:, w]).then_inc(wq_ok, 1)

            def wfc_low():
                dve.wait_ge(w_hi, 4)
                low(wfc_l[:, :, :].rearrange("p c n -> p (c n)"), wfc_raw[:, :],
                    wfc_h[:, :, :].rearrange("p c n -> p (c n)")).then_inc(wfc_ok, 1)

            v.memset(k_st[0:ST, :, :, :].bitcast(f32), 1.0).then_inc(consts, 1)
            statistics(0)
            dve.wait_ge(w_hi, 1)
            v.tensor_tensor(wkv_l[:, :, :, :].rearrange("p a c n -> p (a c n)"), wkv_raw,
                            wkv_h[:, :, :, :].rearrange("p a c n -> p (a c n)").bitcast(f32),
                            ALU.subtract).then_inc(wkv_ok, 1)
            cx_low(0)
            cx_low(1)
            norm_rows(0)
            cx_low(2)
            wq_low(0)
            cx_low(3)
            x_low(0, 0)
            x_low(0, 1)
            wq_low(1)
            x_low(0, 2)
            x_low(0, 3)
            k_low(0)
            statistics(1)
            q_low(0, 0)
            dve.wait_ge(gate_ok, 2)
            v.tensor_scalar(tbias[:, :], tbias[:, :], tgx[:, :], None, ALU.mult).then_inc(tb_ok, 1)
            q_low(0, 1)
            statistics(2)
            q_low(0, 2)
            for u in range(UNITS):
                maximum(0, u, 0)
            for u in range(UNITS):
                maximum(1, u, 1)
            wfc_low()
            q_low(0, 3)
            norm_rows(1)
            v.memset(wr[:, :, :], 0.0).then_inc(wr_ok, 1)
            dve.wait_ge(wr_ok, 1)
            v.tensor_copy(wr[:, :, 0:EXPERTS], wr_raw[:, :].rearrange("p (c e) -> p c e", c=DC)).then_inc(wr_ok, 1)

            def a_low(n, c, last_batch):
                dve.wait_ge(a_hi, n + 1)
                low(a_split(False, last_batch)[:, c, :], aT[:, :], a_split(True, last_batch)[:, c, :]).then_inc(a_lo, 1)

            def norm2_rows(lot, a, b):
                dve.wait_ge(rs2_ok, lot + 1)
                v.scalar_tensor_tensor(nmr[:, 1, a:b], mv[:, 1, a:b, 0], -1.0, rstd[:, 1, a:b],
                                       ALU.mult, ALU.mult).then_inc(nm2_ok, 1)

            def o_turn(n):
                dve.wait_ge(pv_ok, 4 * n + 4)
                v.transpose(oB[:, :, :].rearrange("p b w -> p (b w)"), OTB[:, :]).then_inc(ob_ok, 1)

            def inverse(n):
                dve.wait_ge(ob_ok, n + 1)
                v.reciprocal(rden[:, :], oB[:, :, DH]).then_inc(rden_ok, 1)

            def divide(n):
                dve.wait_ge(rden_ok, n + 1)
                inv = rden[:, :].rearrange("p (g b) -> p g b", g=2).unsqueeze(3).to_broadcast([P, 2, S // VW, DH])
                v.tensor_tensor(oN[:, :, :].rearrange("p b (g d) -> p g b d", g=2),
                                oB[:, :, 0:DH].rearrange("p (g b) d -> p g b d", g=2), inv, ALU.mult).then_inc(norm_ok, 1)
                dve.wait_ge(norm_ok, n + 1)
                if not (isinstance(n, int) and n == 0):
                    dve.wait_ge(a_lo, n)
                v.transpose(aT[:, :], oN[:, :, :].rearrange("p b w -> p (b w)")).then_inc(at_ok, 1)

            def body(t, first, last):
                nx = t + 1
                for s in range(STEPS):
                    n = STEPS * t + s
                    prev = not (first and s == 0)
                    for u in range(UNITS):
                        if not last or s + 2 < STEPS:
                            maximum(n + 2, u, s % 2)
                        if not last and s in (3, 6) and u == 0:
                            q_low(nx, s // 6)
                        if not last and s == 0 and u == 3:
                            x_low(nx, 0)
                        if first and s in (2, 3) and u in (4, 7):
                            dve.wait_ge(in_x[BLOCKS - 1], 16)
                            tile_stats(T // P - TILES + 2 * (s - 2) + u // 7)
                        if first and s == 4 and u == 0:
                            aggregates(BLOCKS - 1)
                        if first and s == 5 and u == 0:
                            norm_rows(2)
                        if prev:
                            if u == 1:
                                o_turn(n - 1)
                            if u == 2:
                                inverse(n - 1)
                            if u == 3:
                                divide(n - 1)
                            if u == split_unit(s) + 1:
                                a_low(n - 1, (s - 1) % CHUNKS, last and s > CHUNKS)
                        if s == 1 and u in (0, 4) and not first:
                            f_sum(t - 1, 1, u // 4)
                        if s in (2, 3) and u == 5 and not first:
                            f_stats(t - 1, 1, s - 2)
                        if s == 5 and u in (0, 5) and not last:
                            f_sum(t, 0, u // 5)
                        if last and (s, u) in ((5, 5), (6, 0)):
                            f_sum(t, 0, s - 5)
                        if s == 7 and u in (1, 4):
                            f_stats(t, 0, u // 4)
                        if last and s == 5 and u == 7:
                            norm2_rows(0, 0, 12)
                        if last:
                            continue
                        if s == 0 and u == 6:
                            x_low(nx, 1)
                        if s == 1 and u == 6:
                            x_low(nx, 2)
                        if s == 2 and u == 0:
                            x_low(nx, 3)
                        if s == 4 and u == 0:
                            k_low(nx)
                        if s in (6, 7) and u == 5:
                            q_low(nx, s - 4)
                    if last and s == 3:
                        dve.wait_ge(ln2_stats, TILES * t)
                        for i in range(TILES * t):
                            aggregate(1, i, ln2_var)

            blocks(dve, body)
            N = STEPS * BLOCKS
            o_turn(N - 1)
            inverse(N - 1)
            divide(N - 1)

            def x2_low(i):
                sl = slice(i * P, (i + 1) * P)
                dve.wait_ge(x2_hi, i + 1)
                low(x2T_l[:, :, sl], x2_bank(i)[:, :].rearrange("p (c q) -> p c q", c=DC),
                    x2T_h[:, :, sl]).then_inc(x2_lo, 1)

            x2_low(0)
            a_low(N - 1, CHUNKS - 1, True)
            for i in range(1, TILES):
                x2_low(i)
            f_sum(BLOCKS - 1, 1, 0)
            f_sum(BLOCKS - 1, 1, 1)
            f_stats(BLOCKS - 1, 1, 0)
            f_stats(BLOCKS - 1, 1, 1)
            dve.wait_ge(ln2_stats, T // P)
            for i in range(12, T // P):
                aggregate(1, i, ln2_var)
            norm2_rows(1, 12, T // P)

            def accumulate(k, b, routed):
                for j in range(TILES):
                    i = TILES * b + j
                    dve.wait_ge(y_full, TILES * k + j + 1)
                    scale = comb[:, 0, i:i + 1] if routed else tgf[:, :]
                    v.scalar_tensor_tensor(xa[:, i, :], bank[4 + j][:, :], scale, xa[:, i, :],
                                           ALU.mult, ALU.add).then_inc(acc_ok, 1)

            def logits():
                dve.wait_ge(lg_mm, 1)
                v.tensor_copy(logT[:, :], bank[4][:, :]).then_inc(lg_cp, 1)

            def top_two():
                dve.wait_ge(lg_tr, 1)
                lg = bank[5][:, :].rearrange("p (j b e) -> p j b e", j=TILES, b=BLOCKS)
                for b in range(BLOCKS):
                    for j in range(TILES):
                        v.max(top[:, TILES * b + j, :], lg[:, j, b, 0:EXPERTS]).then_inc(top_ok, 1)
                dve.wait_ge(top_ok, T // P)
                v.tensor_tensor(comb[:, 0, :], top[:, :, 1], top[:, :, 0], ALU.subtract).then_inc(comb_ok, 1)

            def weights():
                dve.wait_ge(e_ok, 1)
                v.tensor_scalar(comb[:, 2, :], comb[:, 1, :], 1.0, None, ALU.add).then_inc(comb_ok, 1)
                dve.wait_ge(comb_ok, 2)
                v.reciprocal(comb[:, 3, :], comb[:, 2, :]).then_inc(comb_ok, 1)
                dve.wait_ge(comb_ok, 3)
                v.tensor_tensor(comb[:, 1, :], comb[:, 1, :], comb[:, 3, :], ALU.mult).then_inc(comb_ok, 1)
                dve.wait_ge(comb_ok, 4)
                v.tensor_tensor(comb[:, 2, :], comb[:, 1, :], comb[:, 3, :], ALU.add).then_inc(comb_ok, 1)
                dve.wait_ge(comb_ok, 5)
                v.tensor_scalar(comb[:, 0, :], comb[:, 2, :], tgf[:, :], None, ALU.mult).then_inc(comb_ok, 1)
                dve.wait_ge(comb_ok, 6)

            def section(sc, par):
                head = isinstance(sc, int) and sc == 0
                tail = isinstance(sc, int) and sc == SECTIONS - 1
                routing = isinstance(sc, int) and sc == SECTIONS - 2
                for b in range(BLOCKS):
                    k = BLOCKS * sc + b
                    for ic in range(IC):
                        dve.wait_ge(silu_ok, IC * k + ic + 1)
                        if not (head and b == 0):
                            dve.wait_ge(h_lo, IC * (k - 1) + ic + 1)
                        v.tensor_tensor(hid[:, ic, :], bank[2 * ic + 1][:, :], silu[:, ic, :],
                                        ALU.mult).then_inc(hid_ok, 1)
                        if ic == 0 and head and b + 1 < BLOCKS:
                            for i in range(TILES * (b + 1), TILES * (b + 2)):
                                x2_low(i)
                        if ic == 0 and routing and b == 1:
                            top_two()
                    for ic in range(IC):
                        dve.wait_ge(h_hi, IC * k + ic + 1)
                        v.tensor_tensor(hT_l[:, b % 2, ic, :], hid[:, ic, :], hT_h[:, b % 2, ic, :].bitcast(f32),
                                        ALU.subtract).then_inc(h_lo, 1)
                    if not (head and b == 0):
                        accumulate(k - 1, (b - 1) % BLOCKS, tail and b > 0)
                    if routing and b == 0:
                        logits()
                if tail:
                    accumulate(BLOCKS * SECTIONS - 1, BLOCKS - 1, True)

            def section_w(sc, par):
                if isinstance(sc, int) and sc == SECTIONS - 1:
                    weights()
                section(sc, par)

            sections(dve, section_w)

        @block.tensor
        def _(pe):
            mm = nc.tensor.matmul
            N = STEPS * BLOCKS

            def three(out, a_h, a_l, b_h, b_l, start, stop):
                mm(out, a_h, b_l, start=start, stop=False)
                mm(out, a_l, b_h, start=False, stop=False)
                return mm(out, a_h, b_h, start=False, stop=stop)

            def tr(out, in_):
                return nc.tensor.transpose(out, in_, ident[:, :])

            def x_job(tb, j):
                pe.wait_ge(xn_ok, TILES * tb + j + 1)
                for c in range(DC):
                    last = tr(x_bank(tb, j)[:, c * P:(c + 1) * P], xn[:, j, c * P:(c + 1) * P])
                last.then_inc(x_tr, 1)

            def q_part(tb, oc, c):
                if c == 0:
                    pe.wait_ge(x_lo, TILES * (tb + 1))
                w = slice(oc * P, (oc + 1) * P)
                last = three(PJ[(oc + 1) % 2][:, :], wq_h[:, c, w], wq_l[:, c, w], xnT_h[:, c, :], xnT_l[:, c, :],
                             c == 0, c == DC - 1)
                if c == DC - 1:
                    last.then_inc(q_pr, 1)

            def kv_part(tb, a, c):
                pe.wait_ge(cx_split, DC * tb + c + 1)
                last = three(PJ[a][:, :], wkv_h[:, a, c, :], wkv_l[:, a, c, :], cx_h[:, c % 2, :], cx_l[:, c % 2, :],
                             c == 0, c == DC - 1)
                if a == 1:
                    last.then_inc(cx_used, 1)
                elif c == DC - 1:
                    last.then_inc(k_pr, 1)

            def vt_job(tb, bb):
                pe.wait_ge(v_cp, tb + 1)
                for kt in range(S // P):
                    last = tr(PJ[(bb + 1) % 2][:, kt * P:(kt + 1) * P], vT[:, bb * S + kt * P:bb * S + (kt + 1) * P])
                last.then_inc(vt_tr, 1)

            def f_part(t, bb, qt, c, last_batch=False):
                if qt == 0:
                    pe.wait_ge(a_lo, STEPS * t + CHUNKS * bb + c + 1)
                w = slice(qt * P, (qt + 1) * P)
                a_h, a_l = a_split(True, last_batch), a_split(False, last_batch)
                last = three(PJ[qt][:, :], a_h[:, c, w], a_l[:, c, w], wfc_h[:, c, :], wfc_l[:, c, :],
                             c == 0, c == DC - 1)
                if c == DC - 1:
                    last.then_inc(f_mm, 1)

            def sm_unit(n, u, bb, c):
                qt, g2, half = u // 2 % 2, u // 4, u % 2
                banks = sm_banks(n)
                if not (isinstance(n, int) and n == 0 and u < banks):
                    pe.wait_ge(max_ok, UNITS * n + u + 1 - banks)
                for j in range(2):
                    h = g2 * RH + half * 2 + j
                    last = mm(bank[u % banks][:, j * S:(j + 1) * S], q_st[0:SM, c, h, qt * P:(qt + 1) * P],
                              k_st[0:SM, bb, 2 * c + g2, :], start=True, stop=True)
                last.then_inc(sm_full, 1)

            def st_unit(n, u, bb, c):
                g2, kt, half = u // 4, u // 2 % 2, u % 2
                if not (isinstance(n, int) and n == 0 and u < 2):
                    pe.wait_ge(exp_ok, UNITS * n + u - 1)
                h = g2 * RH + half * 2
                mm(STB[u % 2][:, :], k_st[0:ST, bb, 2 * c + g2, kt * P:(kt + 1) * P], q_st[0:ST, c, h:h + 2, :],
                   start=True, stop=True).then_inc(st_full, 1)

            def pv_unit(n, p, bb, c):
                g2, kt = p // 2, p % 2
                pe.wait_ge(exp_ok, UNITS * n + 2 * p + 2)
                if p == 0 and not (isinstance(n, int) and n == 0):
                    pe.wait_ge(ob_ok, n)
                for r in range(RH):
                    last = mm(OTB[32 * r:32 * r + VW, g2 * S:(g2 + 1) * S], vals[:, bb, kt, 2 * c + g2, :],
                              probs[:, p, r, :], start=kt == 0, stop=kt == 1)
                last.then_inc(pv_ok, 1)

            def mt_job(n, par):
                pe.wait_ge(max_ok, UNITS * n + UNITS)
                tr(TPB[0:16, 0:P], mcol[:, par, :]).then_inc(mt_tr, 1)

            def x2_job(i):
                pe.wait_ge(xn2_ok, i + 1)
                if i < 2:
                    pe.wait_ge(max_ok, UNITS * N)
                elif i < 4:
                    pe.wait_ge(exp_ok, UNITS * N)
                elif i < 2 * TILES:
                    done, count = ((ob_ok, N), (mt_cp, N), (f_add, T // P - 1), (f_add, T // P))[i - TILES]
                    pe.wait_ge(done, count)
                elif i < 3 * TILES:
                    pe.wait_ge(x2_lo, i - TILES + 1)
                else:
                    pe.wait_ge(acc_ok, i - 3 * TILES + 1)
                for c in range(DC):
                    last = tr(x2_bank(i)[:, c * P:(c + 1) * P], xn[:, i % 4, c * P:(c + 1) * P])
                last.then_inc(x2_tr, 1)

            pe.wait_ge(ident_ok, 1)
            pe.wait_ge(wkv_ok, 1)
            for c in range(DC):
                kv_part(0, 0, c)
                kv_part(0, 1, c)
                if c > 0:
                    x_job(0, c - 1)
            x_job(0, DC - 1)
            pe.wait_ge(wq_ok, 2)

            def q_job(oc, done, count):
                pe.wait_ge(done, count)
                for c in range(DC):
                    q_part(0, oc, c)

            q_job(0, v_cp, 1)
            q_job(1, k_lo, 1)
            q_job(2, q_lo, 1)
            pe.wait_ge(consts, CONSTS)
            pe.wait_ge(k_rd[0], 48)
            pe.wait_ge(q_rd[0], 48)
            for u in range(UNITS):
                sm_unit(0, u, 0, 0)
            mt_job(0, 0)
            pe.wait_ge(q_lo, 3)
            vt_job(0, 0)
            pe.wait_ge(q_rd[1], 48)
            for u in range(UNITS):
                sm_unit(1, u, 0, 1)
            q_job(3, q_lo, 2)

            def body(t, first, last):
                nx = t + 1
                for s in range(STEPS):
                    n = STEPS * t + s
                    bb, c = s // CHUNKS, s % CHUNKS
                    e = s + 2
                    te = t if e < STEPS else nx
                    be, ce = e % STEPS // CHUNKS, e % CHUNKS
                    look = not last or e < STEPS
                    for u in range(UNITS):
                        if look:
                            if u == 0:
                                pe.wait_ge(q_rd[ce], 48 * (2 * te + be + 1))
                                pe.wait_ge(k_rd[be], 48 * (te + 1))
                            sm_unit(n + 2, u, be, ce)
                        if u == 0:
                            pe.wait_ge(m_rd, 32 * (n + 1))
                        st_unit(n, u, bb, c)
                        if u == 1 and not (first and s == 0):
                            pv_unit(n - 1, 3, (s - 1) % STEPS // CHUNKS, (s - 1) % CHUNKS)
                        if u == 3 and c == 0:
                            pe.wait_ge(vt_cp, 2 * t + bb + 1)
                        if u in (3, 5, 7):
                            pv_unit(n, u // 2 - 1, bb, c)
                        if u == 2 and (not last or s + 1 < STEPS):
                            pe.wait_ge(mt_cp, n + 1)
                            mt_job(n + 1, (s + 1) % 2)
                        part = u % 4
                        if s == 0 and not last:
                            if u == 1:
                                pe.wait_ge(q_lo, CHUNKS * t + 4)
                                x_job(nx, 0)
                            if u == 3:
                                pe.wait_ge(vt_cp, 2 * t + 1)
                                x_job(nx, 1)
                        if s == 0 and u >= 4 and not first:
                            if u == 4 and last:
                                pe.wait_ge(q_lo, CHUNKS * t + 4)
                            if u == 4 and not last:
                                pe.wait_ge(x_lo, TILES * nx + 1)
                            f_part(t - 1, 1, 0, part)
                        if s == 1 and u < 4 and not first:
                            if u == 0 and last:
                                pe.wait_ge(vt_cp, 2 * t + 1)
                            if u == 0 and not last:
                                pe.wait_ge(x_lo, TILES * nx + 2)
                            f_part(t - 1, 1, 1, part)
                        if s == 1 and u in (4, 6) and not last:
                            if first:
                                pe.wait_ge(x_lo, TILES * nx + u // 2 - 1)
                            else:
                                pe.wait_ge(f_add, TILES * t + u // 2 - 3)
                            x_job(nx, u // 2)
                        if s == 2 and u == 1:
                            if last:
                                pe.wait_ge(f_add, TILES * t - 1)
                            else:
                                pe.wait_ge(x_lo, TILES * nx + 3)
                            vt_job(t, 1)
                        if s == 2 and u >= 4 and not last:
                            q_part(nx, 0, part)
                        if s == 3 and not last:
                            if u == 0:
                                pe.wait_ge(vt_cp, 2 * t + 2)
                            if u == 1:
                                pe.wait_ge(q_lo, CHUNKS * nx + 1)
                            kv_part(nx, u % 2, u // 2)
                        if s == 4 and u >= 4 and not last:
                            if u == 4:
                                pe.wait_ge(k_lo, nx + 1)
                            if u == 4 and first:
                                pe.wait_ge(wfc_ok, 1)
                            f_part(t, 0, 0, part)
                        if s == 5 and u < 4 and not last:
                            if u == 0:
                                pe.wait_ge(v_cp, nx + 1)
                            f_part(t, 0, 1, part)
                        if last and 2 <= s < 6 and u in (3, 6):
                            if s == 2:
                                if u == 3:
                                    pe.wait_ge(vt_cp, 2 * t + 2)
                                else:
                                    pe.wait_ge(f_add, TILES * t)
                            f_part(t, 0, u // 6, s - 2)
                        if last and s == 6 and u in (1, 4):
                            pe.wait_ge(f_add, TILES * t + 1 + u // 4)
                            f_part(t, 1, u // 4, 0, True)
                        if last and s == 7 and u in (1, 2):
                            f_part(t, 1, u - 1, 1, True)
                        if last and s == 7 and u in (3, 5):
                            x2_job(u // 5)
                        if s == 5 and u >= 4 and not last:
                            if u == 4:
                                pe.wait_ge(f_add, TILES * t + 1)
                            q_part(nx, 1, part)
                        if s == 6 and u < 4 and not last:
                            if u == 0:
                                pe.wait_ge(f_add, TILES * t + 2)
                            q_part(nx, 2, part)
                        if s == 7 and u < 4 and not last:
                            if u == 0:
                                pe.wait_ge(q_lo, CHUNKS * nx + 2)
                            q_part(nx, 3, part)
                        if s == 7 and u == 5 and not last:
                            pe.wait_ge(q_lo, CHUNKS * nx + 3)
                            vt_job(nx, 0)

            blocks(pe, body)
            for qt in range(2):
                f_part(BLOCKS - 1, 1, qt, DC - 2, True)
            pv_unit(N - 1, 3, 1, CHUNKS - 1)
            x2_job(2)
            x2_job(3)
            for qt in range(2):
                f_part(BLOCKS - 1, 1, qt, DC - 1, True)

            G, U, Y = bank[0:4:2], bank[1:4:2], bank[4:8]

            def gate_up(k, b, par, ic, free):
                if free:
                    pe.wait_ge(hid_ok, IC * (k - 1) + ic + 1)
                tok = slice(b * BLOCK, (b + 1) * BLOCK)
                for o, bk in ((0, G[ic]), (GUW, U[ic])):
                    for c in range(DC):
                        w = slice(o + c * SC + ic * P, o + c * SC + (ic + 1) * P)
                        last = three(bk[:, :], w_h[par][:, w], w_l[par][:, w], x2T_h[:, c, tok], x2T_l[:, c, tok],
                                     c == 0, c == DC - 1)
                last.then_inc(gu_full, 1)

            def down(k, b, par, head):
                pe.wait_ge(h_lo, IC * (k + 1))
                for j in range(TILES):
                    if head and b < 2:
                        pe.wait_ge(x2_lo, TILES * (b + 2) + j + 1)
                    else:
                        pe.wait_ge(acc_ok, TILES * (k - 1) + j + 1)
                    tok = slice(j * P, (j + 1) * P)
                    for ic in range(IC):
                        w = slice(2 * GUW + ic * D, 2 * GUW + (ic + 1) * D)
                        last = three(Y[j][:, :], hT_h[:, b % 2, ic, tok], hT_l[:, b % 2, ic, tok],
                                     w_h[par][:, w], w_l[par][:, w], ic == 0, ic == IC - 1)
                    last.then_inc(y_full, 1)

            def logits(k):
                pe.wait_ge(wr_ok, 2)
                pe.wait_ge(acc_ok, TILES * k + 1)
                for c in range(DC):
                    for part in (x2T_l, x2T_h):
                        for b in range(BLOCKS):
                            last = mm(bank[4][32 * b:32 * b + 32, :], wr[:, c, :],
                                      part[:, c, b * BLOCK:(b + 1) * BLOCK].bitcast(f32),
                                      start=c == 0 and part is x2T_l, stop=c == DC - 1 and part is x2T_h)
                last.then_inc(lg_mm, 1)

            def logits_turn(k):
                pe.wait_ge(lg_cp, 1)
                pe.wait_ge(acc_ok, TILES * k + 2)
                for j in range(TILES):
                    last = tr(bank[5][:, j * P:(j + 1) * P], logT[:, j * P:(j + 1) * P])
                last.then_inc(lg_tr, 1)

            def section(sc, par):
                head = isinstance(sc, int) and sc == 0
                routing = isinstance(sc, int) and sc == SECTIONS - 2
                if head:
                    pe.wait_ge(x2_lo, TILES)
                pe.wait_ge(ffn_w_ok, sc + 1)
                for b in range(BLOCKS):
                    k = BLOCKS * sc + b
                    if head and b > 0:
                        pe.wait_ge(x2_lo, TILES * (b + 1))
                    for ic in range(IC):
                        gate_up(k, b, par, ic, not (head and b == 0))
                        if ic == 0 and head and b + 1 < BLOCKS:
                            for i in range(TILES * (b + 1), TILES * (b + 2)):
                                x2_job(i)
                        if ic == 0 and routing and b == 1:
                            logits_turn(k - 2)
                    if routing and b == 1:
                        pe.wait_ge(top_ok, T // P)
                    if not (head and b == 0):
                        down(k - 1, (b - 1) % BLOCKS, par if b else 1 - par, head)
                    if routing and b == 0:
                        logits(k - 1)

            sections(pe, section)
            down(BLOCKS * SECTIONS - 1, BLOCKS - 1, 0, False)


_OUT = (B, S, D)


def kernel(**inputs):
    import concourse.bacc as bacc
    from concourse.bass_utils import run_bass_kernel_spmd

    def arr(name):
        return np.asarray(inputs[name])

    def rows(w):
        return np.ascontiguousarray(w.T.reshape(w.shape[1] // P, P, w.shape[0]).transpose(1, 0, 2)).reshape(P, -1)

    gate = np.concatenate([arr("L0_ffn_sh_gate"), arr("L0_ffn_r_gate")], 0)
    up = np.concatenate([arr("L0_ffn_sh_up"), arr("L0_ffn_r_up")], 0)
    down = np.concatenate([arr("L0_ffn_sh_down"), arr("L0_ffn_r_down")], 1)
    w_ffn = np.stack([
        np.concatenate([rows(gate[i * SC:(i + 1) * SC]), rows(up[i * SC:(i + 1) * SC]),
                        rows(down[:, i * SC:(i + 1) * SC])], 1) for i in range(SECTIONS)])
    ctx_t = arr("ctx_2048").reshape(BLOCKS, BLOCK, DC, P).transpose(0, 2, 3, 1)
    wfc = arr("L0_xattn_Wfc").T.reshape(DC, 2, RH, DH, D).transpose(2, 1, 3, 0, 4)
    arrays = {
        "x": arr("x").reshape(T, D),
        "ctxT": ctx_t,
        "wq": rows(arr("L0_xattn_Wq")), "wk": rows(arr("L0_xattn_Wk")), "wv": rows(arr("L0_xattn_Wv")),
        "wfc": np.ascontiguousarray(wfc).reshape(P, -1), "bfc": arr("L0_xattn_bfc"),
        "g_x": arr("g_xattn"), "g_f": arr("g_ffn"),
        "w_ffn": w_ffn, "w_r": rows(arr("L0_ffn_router_weight")),
    }
    arrays = {k: np.ascontiguousarray(v) for k, v in arrays.items()}
    nc = bacc.Bacc("TRN2", target_bir_lowering=False, num_devices=1)
    args = {k: nc.dram_tensor(k, v.shape, mybir.dt.from_np(v.dtype), kind="ExternalInput").ap()
            for k, v in arrays.items()}
    out = nc.dram_tensor("out", (T, D), mybir.dt.float32, kind="ExternalOutput").ap()
    build(nc, out=out, **args)
    r = run_bass_kernel_spmd(nc, [arrays], core_ids=[0])
    return r.results[0]["out"].reshape(_OUT)
```
